# Optimizing a Trainium2 kernel written in Bass

```python
import numpy as np
import jax
import jax.numpy as jnp

def _softmax(x, axis=-1):
    return jax.nn.softmax(x, axis=axis)

def _gelu(x):
    return jax.nn.gelu(x, approximate=True)

def _silu(x):
    return jax.nn.silu(x)

def _sigmoid(x):
    return jax.nn.sigmoid(x)

def _layernorm(x, axis=-1, eps=1e-05):
    m = jnp.mean(x, axis=axis, keepdims=True)
    v = jnp.var(x, axis=axis, keepdims=True)
    return (x - m) / jnp.sqrt(v + eps)

def _scatter_add(tgt, idx, src, axis=0):
    return tgt.at[idx].add(src)

def _segment_sum(src, seg, n):
    return jax.ops.segment_sum(src, seg, n)
kernel_name = 'mk_xattn_ffn_d2_seqx_r8_cf616a'

def setup_inputs(seed: int=0):
    np.random.seed(seed)
    _w = jnp.asarray

    def _rec_inputs():
        import jax
        import jax.numpy as jnp
        _rk = jax.random.key(seed)
        x = -7.109e-05 + 0.9999 * jax.random.normal(jax.random.fold_in(_rk, 1), (4, 256, 256), jnp.float32)
        _lenS = 256 - jax.random.randint(jax.random.fold_in(_rk, 7), (4,), 0, max(1, 256 // 4) + 1, jnp.int32)
        _lenS2 = 256 - jax.random.randint(jax.random.fold_in(_rk, 8), (4,), 0, max(1, 256 // 4) + 1, jnp.int32)
        _ctx_512P = jax.random.normal(jax.random.fold_in(_rk, 11), (4, 16, 64), jnp.float32)
        _ctx_512c = jax.random.dirichlet(jax.random.fold_in(_rk, 511), 0.3 * jnp.ones((16,), jnp.float32), (4, 256))
        _ctx_512t = jnp.einsum('bsk,bkd->bsd', _ctx_512c, _ctx_512P)
        _ctx_512t = _ctx_512t * jax.lax.rsqrt(jnp.mean(jnp.square(_ctx_512t)) + 1e-12) * 0.953939
        ctx_512 = 2.81802e-05 + 1.00001 * (_ctx_512t + 0.3 * jax.random.normal(jax.random.fold_in(_rk, 611), (4, 256, 64), jnp.float32))
        return (x, ctx_512)
    x, ctx_512 = _rec_inputs()

    def _L0_xattn_setup():
        import jax, jax.numpy as jnp
        import numpy as np
        EPS = 1e-06
        IMAGE_DIMS = 256
        key = jax.random.key(seed)
        k1, k2, k3 = jax.random.split(key, 3)
        B, I, J, D = (16, 256, 256, 64)
        p = jax.random.normal(k1, (B, I, J), dtype=jnp.float32)
        k_v = jax.random.normal(k2, (B, J, D), dtype=jnp.float32)
        W_k = jax.random.normal(k3, (D, D), dtype=jnp.float32) * (1.0 / np.sqrt(D))
        b_k = jnp.zeros((D,), dtype=jnp.float32)
        ln_gamma = jnp.ones((J,), dtype=jnp.float32)
        ln_beta = jnp.zeros((J,), dtype=jnp.float32)
        return {'p': p, 'k_v': k_v, 'W_k': W_k, 'b_k': b_k, 'ln_gamma': ln_gamma, 'ln_beta': ln_beta}
    _L0_xattn_all = _L0_xattn_setup()
    _L0_xattn_in = {k: v for k, v in _L0_xattn_all.items() if k in ('W_k', 'b_k', 'ln_gamma', 'ln_beta')}
    del _L0_xattn_all

    def _L0_ffn_setup():
        import jax, jax.numpy as jnp
        import numpy as np

        def _sparsify_2to4(h):
            B, S, I = h.shape
            g = h.reshape(B, S, I // 4, 4)
            a = jnp.abs(g)
            _, idx = jax.lax.top_k(a, 2)
            pos = jnp.arange(4)
            mask = (pos == idx[..., 0:1]) | (pos == idx[..., 1:2])
            return (g * mask.astype(g.dtype)).reshape(B, S, I)
        key = jax.random.key(seed)
        k1, k2, k3, k4 = jax.random.split(key, 4)
        B, S, H, I = (4, 256, 256, 1024)
        x = jax.random.normal(k1, (B, S, H), dtype=jnp.float32)
        w_gate = jax.random.normal(k2, (H, I), dtype=jnp.float32) / np.sqrt(H)
        w_up = jax.random.normal(k3, (H, I), dtype=jnp.float32) / np.sqrt(H)
        w_down = jax.random.normal(k4, (I, H), dtype=jnp.float32) / np.sqrt(I)
        return {'x': x, 'w_gate': w_gate, 'w_up': w_up, 'w_down': w_down}
    _L0_ffn_all = _L0_ffn_setup()
    _L0_ffn_in = {k: v for k, v in _L0_ffn_all.items() if k in ('w_gate', 'w_up', 'w_down')}
    del _L0_ffn_all

    def _L1_xattn_setup():
        import jax, jax.numpy as jnp
        import numpy as np
        B, S, L = (2, 128, 128)
        DIM_Q, H, K, D_C, D_CQ, R = (256, 16, 128, 64, 192, 64)

        def _rope_tables(seq_len, dim, dtype):
            inv_freq = 1.0 / 10000.0 ** (jnp.arange(0, dim, 2, dtype=dtype) / dim)
            t = jnp.arange(seq_len, dtype=dtype)
            freqs = t[:, None] * inv_freq[None, :]
            sin = jnp.repeat(jnp.sin(freqs), 2, axis=-1)
            cos = jnp.repeat(jnp.cos(freqs), 2, axis=-1)
            return (sin, cos)

        def _rotate_half(x):
            h = x.shape[-1] // 2
            return jnp.concatenate([-x[..., h:], x[..., :h]], axis=-1)
        key = jax.random.key(seed)
        ks = jax.random.split(key, 8)
        s_in = 1.0 / np.sqrt(DIM_Q)
        s_k = 1.0 / np.sqrt(K)
        s_cq = 1.0 / np.sqrt(D_CQ)
        s_c = 1.0 / np.sqrt(D_C)
        return {'hidden_q': jax.random.normal(ks[0], (B, S, DIM_Q), jnp.float32), 'kv_c': jax.random.normal(ks[1], (B, L, D_C), jnp.float32), 'Wq': jax.random.normal(ks[2], (H * K, DIM_Q), jnp.float32) * s_in, 'w_kc_q': jax.random.normal(ks[3], (H, K, D_CQ), jnp.float32) * s_k, 'w_kc_kv': jax.random.normal(ks[4], (H, K, D_C), jnp.float32) * s_k, 'W_qr': jax.random.normal(ks[5], (H, D_CQ, R), jnp.float32) * s_cq / np.sqrt(R), 'W_kr': jax.random.normal(ks[6], (H, D_C, R), jnp.float32) * s_c, 'Wo': jax.random.normal(ks[7], (DIM_Q, H * K), jnp.float32) * s_k}
    _L1_xattn_all = _L1_xattn_setup()
    _L1_xattn_in = {k: v for k, v in _L1_xattn_all.items() if k in ('Wq', 'w_kc_q', 'w_kc_kv', 'W_qr', 'W_kr', 'Wo')}
    del _L1_xattn_all

    def _L1_ffn_setup():
        import jax, jax.numpy as jnp
        import numpy as np
        TOP_K = 8
        NUM_GROUPS = 8
        key = jax.random.key(seed)
        ks = jax.random.split(key, 6)
        T_B, T_S, H, I, E, G = (1, 256, 256, 96, 32, NUM_GROUPS)
        hidden_states = jax.random.normal(ks[0], (T_B, T_S, H), dtype=jnp.float32)
        gate_weight = jax.random.normal(ks[1], (E, H), dtype=jnp.float32) * 0.02
        gate_up_proj = jax.random.normal(ks[2], (E, 2 * I, H), dtype=jnp.float32) * 0.02
        down_proj = jax.random.normal(ks[3], (E, H, I), dtype=jnp.float32) * 0.02
        merge_groups = jax.random.randint(ks[4], (E,), 0, G, dtype=jnp.int64)
        merge_groups = merge_groups.at[:G].set(jnp.arange(G, dtype=jnp.int64))
        dominant_experts = jax.random.randint(ks[5], (G,), 0, E, dtype=jnp.int64)
        return {'hidden_states': hidden_states, 'gate_weight': gate_weight, 'gate_up_proj': gate_up_proj, 'down_proj': down_proj, 'merge_groups': merge_groups, 'dominant_experts': dominant_experts}
    _L1_ffn_all = _L1_ffn_setup()
    _L1_ffn_in = {k: v for k, v in _L1_ffn_all.items() if k in ('gate_weight', 'gate_up_proj', 'down_proj', 'merge_groups', 'dominant_experts')}
    del _L1_ffn_all
    return {'x': x, 'ctx_512': ctx_512, 'L0_xattn_W_k': _L0_xattn_in['W_k'], 'L0_xattn_b_k': _L0_xattn_in['b_k'], 'L0_xattn_ln_gamma': _L0_xattn_in['ln_gamma'], 'L0_xattn_ln_beta': _L0_xattn_in['ln_beta'], 'L0_ffn_w_gate': _L0_ffn_in['w_gate'], 'L0_ffn_w_up': _L0_ffn_in['w_up'], 'L0_ffn_w_down': _L0_ffn_in['w_down'], 'L1_xattn_Wq': _L1_xattn_in['Wq'], 'L1_xattn_w_kc_q': _L1_xattn_in['w_kc_q'], 'L1_xattn_w_kc_kv': _L1_xattn_in['w_kc_kv'], 'L1_xattn_W_qr': _L1_xattn_in['W_qr'], 'L1_xattn_W_kr': _L1_xattn_in['W_kr'], 'L1_xattn_Wo': _L1_xattn_in['Wo'], 'L1_ffn_gate_weight': _L1_ffn_in['gate_weight'], 'L1_ffn_gate_up_proj': _L1_ffn_in['gate_up_proj'], 'L1_ffn_down_proj': _L1_ffn_in['down_proj'], 'L1_ffn_merge_groups': _L1_ffn_in['merge_groups'], 'L1_ffn_dominant_experts': _L1_ffn_in['dominant_experts']}

def reference(x, ctx_512, L0_xattn_W_k, L0_xattn_b_k, L0_xattn_ln_gamma, L0_xattn_ln_beta, L0_ffn_w_gate, L0_ffn_w_up, L0_ffn_w_down, L1_xattn_Wq, L1_xattn_w_kc_q, L1_xattn_w_kc_kv, L1_xattn_W_qr, L1_xattn_W_kr, L1_xattn_Wo, L1_ffn_gate_weight, L1_ffn_gate_up_proj, L1_ffn_down_proj, L1_ffn_merge_groups, L1_ffn_dominant_experts):
    import jax
    import jax.numpy as jnp

    def _L0_xattn_ref(p, k_v, W_k, b_k, ln_gamma, ln_beta):
        import jax, jax.numpy as jnp
        import numpy as np
        EPS = 1e-06
        IMAGE_DIMS = 256
        kv = k_v @ W_k.T + b_k
        out = jnp.einsum('bij,bjd->bid', p, kv)
        scale = IMAGE_DIMS ** (-0.5)
        sim = jnp.einsum('bid,bjd->bij', out, kv) * scale
        mu = jnp.mean(sim, axis=-1, keepdims=True)
        var = jnp.var(sim, axis=-1, keepdims=True)
        sim = (sim - mu) * jax.lax.rsqrt(var + EPS) * ln_gamma + ln_beta
        attn = jax.nn.softmax(sim, axis=-1)
        return attn

    def _L0_ffn_ref(x, w_gate, w_up, w_down):
        import jax, jax.numpy as jnp
        import numpy as np

        def _sparsify_2to4(h):
            B, S, I = h.shape
            g = h.reshape(B, S, I // 4, 4)
            a = jnp.abs(g)
            _, idx = jax.lax.top_k(a, 2)
            pos = jnp.arange(4)
            mask = (pos == idx[..., 0:1]) | (pos == idx[..., 1:2])
            return (g * mask.astype(g.dtype)).reshape(B, S, I)
        h = jax.nn.silu(jnp.einsum('bsh,hi->bsi', x, w_gate)) * jnp.einsum('bsh,hi->bsi', x, w_up)
        h_sparse = _sparsify_2to4(h)
        return jnp.einsum('bsi,ih->bsh', h_sparse, w_down)

    def _L1_xattn_ref(hidden_q, kv_c, Wq, w_kc_q, w_kc_kv, W_qr, W_kr, Wo):
        import jax, jax.numpy as jnp
        import numpy as np
        B, S, L = (2, 128, 128)
        DIM_Q, H, K, D_C, D_CQ, R = (256, 16, 128, 64, 192, 64)

        def _rope_tables(seq_len, dim, dtype):
            inv_freq = 1.0 / 10000.0 ** (jnp.arange(0, dim, 2, dtype=dtype) / dim)
            t = jnp.arange(seq_len, dtype=dtype)
            freqs = t[:, None] * inv_freq[None, :]
            sin = jnp.repeat(jnp.sin(freqs), 2, axis=-1)
            cos = jnp.repeat(jnp.cos(freqs), 2, axis=-1)
            return (sin, cos)

        def _rotate_half(x):
            h = x.shape[-1] // 2
            return jnp.concatenate([-x[..., h:], x[..., :h]], axis=-1)
        b, s, _ = hidden_q.shape
        l = kv_c.shape[1]
        q_hk = (hidden_q @ Wq.T).reshape(b, s, H, K)
        q_big = jnp.einsum('bshk,hkq->bshq', q_hk, w_kc_q)
        sin, cos = _rope_tables(l, D_C, kv_c.dtype)
        kv_rope = kv_c * cos[None] + _rotate_half(kv_c) * sin[None]
        q_r = jnp.einsum('bshq,hqr->bhsr', q_big, W_qr)
        k_r = jnp.einsum('bld,hdr->bhlr', kv_rope, W_kr)
        scores = jnp.einsum('bhsr,bhlr->bhsl', q_r, k_r)
        attn = jax.nn.softmax(scores, axis=-1)
        ctx_c = jnp.einsum('bhsl,bld->bhsd', attn, kv_rope)
        ctx_lat = jnp.einsum('bhsd,hkd->bshk', ctx_c, w_kc_kv)
        out = ctx_lat.reshape(b, s, H * K) @ Wo.T
        return out

    def _L1_ffn_ref(hidden_states, gate_weight, gate_up_proj, down_proj, merge_groups, dominant_experts):
        import jax, jax.numpy as jnp
        import numpy as np
        TOP_K = 8
        NUM_GROUPS = 8
        B, S, H = hidden_states.shape
        G = dominant_experts.shape[0]
        x = hidden_states.reshape(-1, H)
        logits = jnp.einsum('th,eh->te', x, gate_weight)
        probs = jax.nn.softmax(logits.astype(jnp.float32), axis=-1).astype(logits.dtype)
        top_val, top_idx = jax.lax.top_k(probs, TOP_K)
        top_val = top_val / jnp.sum(top_val, axis=-1, keepdims=True)
        sel_group = merge_groups[top_idx]
        onehot = jax.nn.one_hot(sel_group, G, dtype=top_val.dtype)
        w_tg = jnp.einsum('tk,tkg->tg', top_val, onehot)
        gu = gate_up_proj[dominant_experts]
        dn = down_proj[dominant_experts]
        h = jnp.einsum('th,goh->tgo', x, gu)
        gate, up = jnp.split(h, 2, axis=-1)
        act = jax.nn.silu(gate) * up
        y = jnp.einsum('tgi,ghi->tgh', act, dn)
        out = jnp.einsum('tg,tgh->th', w_tg, y)
        return out.reshape(B, S, H)
    x = x + _L0_xattn_ref(_layernorm(x, axis=-1), ctx_512, L0_xattn_W_k, L0_xattn_b_k, L0_xattn_ln_gamma, L0_xattn_ln_beta)
    x = x + _L0_ffn_ref(_layernorm(x, axis=-1), L0_ffn_w_gate, L0_ffn_w_up, L0_ffn_w_down)
    x = x + _L1_xattn_ref(_layernorm(x, axis=-1), ctx_512, L1_xattn_Wq, L1_xattn_w_kc_q, L1_xattn_w_kc_kv, L1_xattn_W_qr, L1_xattn_W_kr, L1_xattn_Wo)
    x = x + _L1_ffn_ref(_layernorm(x, axis=-1), L1_ffn_gate_weight, L1_ffn_gate_up_proj, L1_ffn_down_proj, L1_ffn_merge_groups, L1_ffn_dominant_experts)
    return x

_drawn_inputs = setup_inputs


def setup_inputs(seed=0):
    import zlib

    import numpy as np

    out = dict(_drawn_inputs(seed))
    spreads = {'L0_xattn_b_k': (0.0, 0.8),
     'L0_xattn_ln_gamma': (1.0, 0.6),
     'L0_xattn_ln_beta': (0.0, 0.8)}
    factors = {'L0_xattn_W_k': 8.0,
     'L1_ffn_gate_weight': 8.0,
     'L1_ffn_gate_up_proj': 8.0,
     'L1_ffn_down_proj': 8.0}
    for name, (base, spread) in spreads.items():
        noise = np.random.default_rng([zlib.crc32(name.encode()), seed]).standard_normal(out[name].shape)
        drawn = base * np.exp(spread * noise) if base else spread * noise
        out[name] = jnp.asarray(drawn.astype(out[name].dtype))
    for name, factor in factors.items():
        out[name] = (out[name] * factor).astype(out[name].dtype)
    return out
```

```python
from contextlib import ExitStack

import numpy as np

import concourse.bass as bass
from concourse import mybir

P = 128
NB = 4
S = 256
TT = 2
D = 256
DC = 64
FFN = 1024
NH = 16
HK = 128
DQ = 192
NP = NH // 2
NE = 32
NG = 8
EI = 96
GC = NG * EI
WM = NE + 2 * GC
UNITS = NB * 8
STEPS = UNITS + 6
LN_EPS = 1e-5
SIM_EPS = 1e-6 * D

ALU = mybir.AluOpType
ACT = mybir.ActivationFunctionType
AX = mybir.AxisListType
F32 = mybir.dt.float32
F32R = mybir.dt.float32r
BF16 = mybir.dt.bfloat16
I32 = mybir.dt.int32


def misc_order():
    order = [("T", 0), ("T", 1), ("T", 2), ("T", 3), ("T", 4), ("T", 5)]
    order += [("T", 6), ("T", 7), ("T", 8), ("T", 9), ("T", 10)]
    for u in range(STEPS):
        if u < 24:
            order.append(("Q", u // 8 + 1, u % 8))
        if u in (8, 16, 24):
            order.append(("T", 10 + u // 8))
        if u % 8 in (4, 5) and u > 8:
            order.append(("O", u // 8 - 1, u % 8 - 4))
    return order + [("T", 14), ("T", 15)]


def two_layers(nc, ins, out):
    MISC = {use: i for i, use in enumerate(misc_order())}

    with ExitStack() as ctx:
        def sb(name, shape, dt=F32, stack=ctx):
            return stack.enter_context(nc.sbuf_tensor(name, shape, dt))

        def sem(name):
            return ctx.enter_context(nc.semaphore(name))

        def overlay(*sets):
            def size(spec):
                n = 2 if spec[2] == BF16 else 4
                for k in spec[1][1:]:
                    n *= k
                return n
            most = max(sum(map(size, s)) for s in sets)
            tiles = {}
            for i, s in enumerate(sets):
                stack = ExitStack() if i < len(sets) - 1 else ctx
                for spec in s:
                    tiles[spec[0]] = sb(*spec, stack=stack)
                if stack is not ctx:
                    stack.close()
                elif (pad := most - sum(map(size, s))) > 0:
                    sb(f"pad_{s[0][0]}", [P, pad // 4], F32)
            return tiles

        X = sb("X", [P, NB * TT, D])
        XN = sb("XN", [P, TT, D])
        XH = sb("XH", [P, 2, 2, S], F32R)
        XL = sb("XL", [P, 2, 2, S], F32R)
        WH = sb("WH", [P, 2 * 2 * FFN], F32R)
        WL = sb("WL", [P, 2 * 2 * FFN], F32R)
        MH = sb("MH", [P, 2, NH * DC], F32R)
        ML = sb("ML", [P, 2, NH * DC], F32R)
        NN = sb("NN", [P, NP, D])
        KRH = sb("KRH", [P, NB * S], F32R)
        KRL = sb("KRL", [P, NB * S], F32R)
        KVN = sb("KVN", [P, NB * TT, DC])
        ident = sb("ident", [P, P])
        st6 = sb("st6", [P, TT, 6])
        st6s = sb("st6s", [P, TT, 6])
        mv = sb("mv", [P, 2, TT, 2])
        mvs = sb("mvs", [P, 2, TT, 2])
        var_eps = sb("var_eps", [P, TT])
        rstd = sb("rstd", [P, 2, TT])
        rstds = sb("rstds", [P, 2, TT])
        half = sb("half", [P, TT])
        negmax = sb("negmax", [P, 4, 4])
        rowsum = sb("rowsum", [P, 4, 4])
        rowrcp = sb("rowrcp", [P, 4, 4])
        dom = sb("dom", [1, NG], I32)
        mg = sb("mg", [P, NE], I32)

        r1 = overlay([("wq", [P, NH, D], F32), ("kcq", [P, NH, DQ], F32), ("qr", [P, 2, NH, DC], F32)],
                     [("qS0", [P, NH, S], F32R), ("qS1", [P, NH, S], F32R)])
        r2 = overlay([("woT", [P, NH, D], F32)],
                     [("ctx0", [P, NP, S], F32), ("ctx1", [P, NP, S], F32)])
        r3 = overlay([("ctxA", [P, NB * S], F32), ("KTH", [P, NB * S], F32R), ("KTL", [P, NB * S], F32R),
                      ("KVH", [P, NB * TT, P], F32R), ("KVL", [P, NB * TT, P], F32R),
                      ("lat", [P, 2, 2, D], F32)],
                     [("kT", [P, NB * S], F32), ("kTrot", [P, NB * S], F32), ("cosT", [P, S], F32),
                      ("sinT", [P, S], F32), ("kN", [P, NB * TT, DC], F32), ("kNrot", [P, NB * TT, DC], F32),
                      ("cosN", [P, TT, DC], F32), ("sinN", [P, TT, DC], F32)],
                     [("P0", [P, 4, S], F32), ("P1", [P, 4, S], F32),
                      ("PT0", [P, 2, 4, S], F32), ("PT1", [P, 2, 4, S], F32)])
        r4 = overlay([("stage", [P, 2 * 2 * FFN], F32), ("Esb", [P, D], F32)],
                     [("hb0", [P, 4, S], F32), ("hb1", [P, 4, S], F32), ("hb2", [P, 4, S], F32),
                      ("hb3", [P, 4, S], F32), ("ab", [P, 4, S], F32), ("g1", [P, 2, S], BF16),
                      ("g2", [P, 2, S], BF16), ("g3", [P, 2, S], BF16), ("e2", [P, 2, S], BF16),
                      ("f2", [P, 2, S], BF16), ("wins", [P, 4, S], BF16)],
                     [("stageM", [P, 2, WM], F32), ("sg0", [P, 2, 384], F32), ("sg1", [P, 2, 384], F32),
                      ("act0", [P, GC], F32), ("act1", [P, GC], F32),
                      ("actT0", [P, 6, P], F32), ("actT1", [P, 6, P], F32)])
        r5 = overlay([("krB", [P, NP, P], F32), ("kckv", [P, NH, DC], F32)],
                     [("wd", [P, 8, D], F32)],
                     [("dnT", [P, 6, D], F32)])
        r6 = overlay([("simn", [P, TT, S], F32), ("gamma", [P, S], F32), ("beta", [P, S], F32), ("outS", [P, S], F32R)],
                     [("onehot", [P, NG, NE], F32), ("pgrp", [P, NG, NE], F32),
                      ("prob", [P, 2, NE], F32), ("left", [P, NE], F32), ("psel", [P, NE], F32)])
        WkA = sb("WkA", [P, P])
        mx8 = sb("mx8", [P, 8])
        rneg = sb("rneg", [P, 1])
        top8 = sb("top8", [P, 8])
        wsum = sb("wsum", [P, NG])
        tsum = sb("tsum", [P, 1])
        trcp = sb("trcp", [P, 1])
        wtg = sb("wtg", [P, NG])

        simn, gamma, beta, outS = (r6[k] for k in ("simn", "gamma", "beta", "outS"))
        onehot, pgrp, prob, left, psel = (r6[k] for k in ("onehot", "pgrp", "prob", "left", "psel"))
        wq, kcq, qr = r1["wq"], r1["kcq"], r1["qr"]
        qS = [r1["qS0"], r1["qS1"]]
        woT, ctxT = r2["woT"], [r2["ctx0"], r2["ctx1"]]
        ctxA, KTH, KTL, KVH, KVL, lat = (r3[k] for k in ("ctxA", "KTH", "KTL", "KVH", "KVL", "lat"))
        Pb, PT = [r3["P0"], r3["P1"]], [r3["PT0"], r3["PT1"]]
        stage = r4["stage"]
        kT, kTrot, cosT, sinT, kN, kNrot, cosN, sinN = (
            r3[k] for k in ("kT", "kTrot", "cosT", "sinT", "kN", "kNrot", "cosN", "sinN"))
        Esb = r4["Esb"]
        hb = [r4[f"hb{i}"] for i in range(4)]
        ab, g1, g2, g3, e2, f2, wins = (r4[k] for k in ("ab", "g1", "g2", "g3", "e2", "f2", "wins"))
        stageM, sg, actb, actT = r4["stageM"], [r4["sg0"], r4["sg1"]], [r4["act0"], r4["act1"]], [r4["actT0"], r4["actT1"]]
        krB, kckv, wd, dnT = r5["krB"], r5["kckv"], r5["wd"], r5["dnT"]

        bank = ctx.enter_context(nc.psum_tensor("bank", [P, 8, 512], F32))

        ld_x = [sem(f"ld_x{b}") for b in range(NB)]
        ld_kv, ld_gb, ld_rope, ld_wgu, ld_wd, ld_moe, ld_dn, ld_idx, ld_id = (
            sem(f"ld_{k}") for k in ("kv", "gb", "rope", "wgu", "wd", "moe", "dn", "idx", "id"))
        ld_fold = [sem(f"ld_fold{c}") for c in range(4)]
        q0_low = sem("q0_low")
        stored = sem("stored")
        dve_step, pool_step = sem("dve_step"), sem("pool_step")
        ln_stats, ln_rstd, ln_norm, ln_T, ln_hi = (sem(k) for k in ("ln_stats", "ln_rstd", "ln_norm", "ln_T", "ln_hi"))
        misc_done = sem("misc_done")
        x_done = sem("x_done")
        kvT_ready, kvT_hi, kvT_lo, kv_ready, kv_hi, kv_lo = (
            sem(k) for k in ("kvT_ready", "kvT_hi", "kvT_lo", "kv_ready", "kv_hi", "kv_lo"))
        out_ready, out_hi, out_lo, sim_ready, sim_stats, sim_rstd, sim_max, sim_exp = (
            sem(k) for k in ("out_ready", "out_hi", "out_lo", "sim_ready", "sim_stats", "sim_rstd", "sim_max", "sim_exp"))
        fD, fD_out, fE, fE_out, fM, fM_hi, fM_lo, fN, fN_out = (
            sem(k) for k in ("fD", "fD_out", "fE", "fE_out", "fM", "fM_hi", "fM_lo", "fN", "fN_out"))
        w_hi, w_lo, ffn_G, ffn_U, ffn_silu, ffn_h, ffn_abs, ffn_cmp, ffn_hs, ffn_D = (
            sem(k) for k in ("w_hi", "w_lo", "ffn_G", "ffn_U", "ffn_silu", "ffn_h", "ffn_abs", "ffn_cmp", "ffn_hs", "ffn_D"))
        q_ready, q_hi, sc_ready, sc_max, p_exp, p_rcp, p_norm, pt_ready, pt_out0, pt_out1, pv_ready, ctx_out, o_ready, rope_done = (
            sem(k) for k in ("q_ready", "q_hi", "sc_ready", "sc_max", "p_exp", "p_rcp", "p_norm", "pt_ready",
                             "pt_out0", "pt_out1", "pv_ready", "ctx_out", "o_ready", "rope_done"))
        m_hi, m_lo, g_ready, u_ready, r_max, r_exp, m_silu, m_act, at_ready, at_out, dn_ready, x_out = (
            sem(k) for k in ("m_hi", "m_lo", "g_ready", "u_ready", "r_max", "r_exp", "m_silu", "m_act",
                             "at_ready", "at_out", "dn_ready", "x_out"))

        WHm = WH[:, 0:2 * WM].rearrange("p (t c) -> p t c", t=2)
        WLm = WL[:, 0:2 * WM].rearrange("p (t c) -> p t c", t=2)
        WHf = WH[:, :].rearrange("p (t s k m) -> p t s k m", t=2, s=2, k=4)
        WLf = WL[:, :].rearrange("p (t s k m) -> p t s k m", t=2, s=2, k=4)

        def f32(ap):
            return ap.bitcast(F32)

        def xin_done(eng, n):
            b = n % 4
            for stage_, s_, count in ((0, out_ready, b + 1), (1, ffn_U, 2 * b + 2), (2, q_ready, 8 * b + 8),
                                      (3, u_ready, 2 * b + 2)):
                if n // 4 == stage_:
                    eng.wait_ge(s_, count)

        block = ctx.enter_context(nc.Block())

        @block.sync
        def _(sp):
            sp.dma_start(ctxA[0:65, :], ins["ctxA"]).then_inc(ld_kv, 16)
            sp.dma_start(WkA[0:65, :], ins["WkA"]).then_inc(ld_kv, 16)
            sp.dma_start(ident[:, :], ins["ident"]).then_inc(ld_id, 16)
            for b in range(NB):
                sp.dma_start(X[:, 2 * b:2 * b + 2, :], ins["x"][b].rearrange("(t p) d -> p t d", p=P)).then_inc(ld_x[b], 16)
            sp.dma_start(gamma[:, :], ins["gamma"].partition_broadcast(P)).then_inc(ld_gb, 16)
            sp.dma_start(beta[:, :], ins["beta"].partition_broadcast(P)).then_inc(ld_gb, 16)
            for c in range(4):
                hs = slice(4 * c, 4 * c + 4)
                for tile, name in ((kcq, "kcq"), (wq, "wq"), (kckv, "kckv"), (woT, "woT")):
                    sp.dma_start(tile[:, hs], ins[name][:, hs]).then_inc(ld_fold[c], 16)
                sp.dma_start(qr[0:96, :, hs], ins["qr"][:, :, hs]).then_inc(ld_fold[c], 16)
                sp.dma_start(krB[:, 2 * c:2 * c + 2], ins["krB"][:, 2 * c:2 * c + 2]).then_inc(ld_fold[c], 16)
            sp.dma_start(stage[:], ins["wgu"]).then_inc(ld_wgu, 16)
            sp.dma_start(dom[:, :], ins["dom"]).then_inc(ld_idx, 16)
            sp.dma_start(mg[:, :], ins["mg"].partition_broadcast(P)).then_inc(ld_idx, 16)
            sp.wait_ge(fM, NP)
            sp.wait_ge(fN, NP)
            sp.dma_start(wd[:], ins["wd"]).then_inc(ld_wd, 16)
            for tile, name in ((kT, "kT"), (kTrot, "kTrot"), (cosT, "cosT"), (sinT, "sinT"), (kN, "kN"),
                               (kNrot, "kNrot"), (cosN, "cosN"), (sinN, "sinN")):
                sp.dma_start(tile[:], ins[name]).then_inc(ld_rope, 16)
            sp.wait_ge(ld_idx, 32)
            expert = [sp.value_load(dom[0:1, g:g + 1], min_val=0, max_val=NE - 1) for g in range(NG)]
            sp.wait_ge(x_done, 8)
            for t in range(2):
                sp.dma_start(stageM[:, t, 0:NE], ins["gwT"][:, t, :]).then_inc(ld_moe, 16)
            for g in range(NG):
                for s in range(2):
                    at = NE + s * GC + g * EI
                    sp.dma_start(stageM[:, :, at:at + EI],
                                 ins["gup"][bass.ds(expert[g], 1), s].rearrange("a p t c -> p (a t) c")).then_inc(ld_moe, 16)
            for g in range(NG):
                done = 0
                while done < EI:
                    row = g * EI + done
                    k = min(EI - done, P - row % P)
                    sp.dma_start(dnT[row % P:row % P + k, row // P, :],
                                 ins["dn"][bass.ds(expert[g], 1), done:done + k].rearrange("a i d -> (a i) d")).then_inc(ld_dn, 16)
                    done += k
            for t in range(NB * TT):
                sp.wait_ge(x_out, t + 1)
                sp.dma_start(out[t // 2, (t % 2) * P:(t % 2 + 1) * P, :], X[:, t, :]).then_inc(stored, 16)
            sp.wait_ge(stored, 16 * NB * TT)

        N_DN = sum(len({(g * EI) // P, (g * EI + EI - 1) // P}) for g in range(NG))

        @block.gpsimd
        def _(pool):
            step = [0]

            def link(ins_):
                step[0] += 1
                ins_.then_inc(pool_step, 1)
                pool.wait_ge(pool_step, step[0])

            link(pool.memset(half[:], -0.5))

            def ln(n):
                pool.wait_ge(ln_stats, n + 1)
                link(pool.tensor_scalar(var_eps[:], mv[:, n % 2, :, 1], LN_EPS, 1.0, ALU.add, ALU.mult))
                pool.tensor_tensor(rstd[:, n % 2, :], var_eps[:], half[:], ALU.pow).then_inc(ln_rstd, 1)
                pool.wait_ge(ln_rstd, n + 1)

            def sim(b):
                pool.wait_ge(sim_stats, b + 1)
                link(pool.tensor_scalar(var_eps[:], mvs[:, b % 2, :, 1], SIM_EPS, 1.0, ALU.add, ALU.mult))
                pool.tensor_tensor(rstds[:, b % 2, :], var_eps[:], half[:], ALU.pow).then_inc(sim_rstd, 1)
                pool.wait_ge(sim_rstd, b + 1)

            ln(0)
            ln(1)
            for b in range(NB):
                ln(b + 2)
                sim(b)
            ln(6)
            pool.wait_ge(ld_rope, 16 * 8)
            kT4 = kT[:].rearrange("p (b l) -> p b l", b=NB)
            kTrot4 = kTrot[:].rearrange("p (b l) -> p b l", b=NB)
            kN4 = kN[:].rearrange("p (b t) d -> p b t d", b=NB)
            kNrot4 = kNrot[:].rearrange("p (b t) d -> p b t d", b=NB)
            for t in range(TT):
                for tab, dst in ((cosN, kN4), (sinN, kNrot4)):
                    link(pool.tensor_tensor(dst[:, :, t, :], dst[:, :, t, :],
                                            tab[:, t, :].unsqueeze(1).broadcast_to([P, NB, DC]), ALU.mult))
            link(pool.tensor_tensor(KVN[:], kN[:], kNrot[:], ALU.add))
            link(pool.tensor_tensor(kT4, kT4, cosT[:, :].unsqueeze(1).broadcast_to([P, NB, S]), ALU.mult))
            link(pool.tensor_tensor(kTrot4, kTrot4, sinT[:, :].unsqueeze(1).broadcast_to([P, NB, S]), ALU.mult))
            ln(7)
            link(pool.tensor_tensor(kT[:], kT[:], kTrot[:], ALU.add))
            link(pool.tensor_copy(KRH[:], kT[:]))
            pool.tensor_tensor(KRL[:], kT[:], f32(KRH[:]), ALU.subtract).then_inc(rope_done, 1)
            for n in range(8, 11):
                ln(n)

            def scale(u):
                pool.wait_ge(p_rcp, u + 1)
                for h in range(4):
                    last = pool.tensor_scalar(Pb[u % 2][:, h, :], Pb[u % 2][:, h, :], rowrcp[:, u % 4, h:h + 1], 1.0,
                                              ALU.mult, ALU.mult)
                last.then_inc(p_norm, 1)

            for u in range(STEPS):
                if 1 <= u <= UNITS:
                    scale(u - 1)
                if u in (6, 14, 22, 30):
                    ln(11 + u // 8)
            ln(15)

        @block.scalar
        def _(act):
            def ln_high(n):
                act.wait_ge(ln_T, n + 1)
                if n >= 2:
                    xin_done(act, n - 2)
                act.activation(XH[:, n % 2, :, :], bank[:, 7, :].rearrange("p (t s) -> p t s", t=2),
                               ACT.Copy).then_inc(ln_hi, 1)

            for c in range(2):
                act.wait_ge(kvT_ready, c + 1)
                act.activation(KTH[:, c * 512:(c + 1) * 512], bank[:, c, :], ACT.Copy).then_inc(kvT_hi, 1)
            for c in range(2):
                act.wait_ge(kv_ready, c + 1)
                act.activation(KVH[:, 4 * c:4 * c + 4, :], bank[:, 2 + c, :].rearrange("p (g d) -> p g d", g=4),
                               ACT.Copy).then_inc(kv_hi, 1)
            def fold_out(i):
                if i < NP:
                    for c in range(2):
                        act.wait_ge(fD, 2 * i + c + 1)
                        if i >= 1:
                            act.wait_ge(fE, i)
                        act.activation(lat[0:96, c, :, :], bank[0:96, c, :].rearrange("p (j d) -> p j d", j=2),
                                       ACT.Copy).then_inc(fD_out, 1)
                    act.wait_ge(fN, i + 1)
                    act.activation(NN[:, i, :], bank[:, 6, 0:D], ACT.Copy).then_inc(fN_out, 1)
                if i >= 1:
                    act.wait_ge(fM, i)
                    act.activation(MH[:, :, (i - 1) * P:i * P], bank[:, 3, 0:2 * P].rearrange("p (t d) -> p t d", t=2),
                                   ACT.Copy).then_inc(fM_hi, 1)

            ln_high(0)
            ln_high(1)
            def sim_softmax(b):
                act.wait_ge(sim_max, b + 1)
                for it in range(TT):
                    last = act.activation(simn[:, it, :], simn[:, it, :], ACT.Exp, bias=negmax[:, b % 4, it:it + 1],
                                          accum_out=rowsum[:, b % 4, it:it + 1])
                last.then_inc(sim_exp, 1)

            def w_high(i):
                if i == 0:
                    act.wait_ge(ld_wgu, 16)
                act.activation(WH[:, i * 1024:(i + 1) * 1024], stage[:, i * 1024:(i + 1) * 1024],
                               ACT.Copy).then_inc(w_hi, 1)

            for b in range(NB):
                act.wait_ge(out_ready, b + 1)
                if b >= 1:
                    act.wait_ge(sim_ready, b)
                act.activation(outS[:, :], bank[:, 4, 0:S], ACT.Copy).then_inc(out_hi, 1)
                if b >= 1:
                    sim_softmax(b - 1)
                fold_out(2 * b)
                ln_high(b + 2)
                if b == 3:
                    w_high(0)
                    w_high(1)
                fold_out(2 * b + 1)
            sim_softmax(NB - 1)
            w_high(2)
            w_high(3)
            fold_out(NP)

            for u in range(8):
                b = u // 2
                act.wait_ge(ffn_G, u + 1)
                if b >= 2:
                    act.wait_ge(ffn_D, b - 1)
                act.activation(hb[u % 4][:], bank[:, 2 * (u % 2):2 * (u % 2) + 2, :].rearrange("p a (k s) -> p (a k) s", k=2),
                               ACT.Silu).then_inc(ffn_silu, 1)
                act.wait_ge(ffn_h, u + 1)
                if u >= 1:
                    act.wait_ge(ffn_cmp, u)
                act.activation(ab[:], hb[u % 4][:], ACT.Abs).then_inc(ffn_abs, 1)
                if u % 2 == 1:
                    ln_high(6 + u // 2)

            def q_high(b, pr):
                act.wait_ge(q_ready, 8 * b + pr + 1)
                if b >= 2:
                    act.wait_ge(sc_ready, 8 * (b - 1))
                at = 7 if b else pr % 4
                act.activation(qS[b % 2][0:64, 2 * pr, :], bank[0:64, at, 0:S], ACT.Copy)
                act.activation(qS[b % 2][64:128, 2 * pr + 1, :], bank[64:128, at, 0:S], ACT.Copy).then_inc(q_hi, 1)

            for pr in range(NP):
                q_high(0, pr)
            ln_high(10)
            for u in range(STEPS):
                if 2 <= u <= UNITS + 1:
                    v = u - 2
                    act.wait_ge(pt_ready, 2 * v + 2)
                    if v // 2 >= 2:
                        act.wait_ge(pv_ready, v // 2 - 1)
                    act.activation(PT[v // 2 % 2][:, 1, :, (v % 2) * P:(v % 2 + 1) * P],
                                   bank[:, 5, :].rearrange("p (h s) -> p h s", h=4), ACT.Copy).then_inc(pt_out1, 1)
                if u < 24:
                    q_high(u // 8 + 1, u % 8)
                if u in (8, 16, 24):
                    ln_high(10 + u // 8)
                if u < UNITS:
                    act.wait_ge(sc_max, u + 1)
                    for h in range(4):
                        last = act.activation(Pb[u % 2][:, h, :], bank[:, 2 * (u % 2) + h // 2, (h % 2) * S:(h % 2 + 1) * S],
                                              ACT.Exp, bias=negmax[:, u % 4, h:h + 1], accum_out=rowsum[:, u % 4, h:h + 1])
                    last.then_inc(p_exp, 1)
                if u in (4, 5, 6, 7):
                    c = u - 4
                    if c == 0:
                        act.wait_ge(ld_moe, 16 * 18)
                    t, a = c // 2, (c % 2) * (WM // 2)
                    act.activation(WHm[:, t, a:a + WM // 2], stageM[:, t, a:a + WM // 2], ACT.Copy).then_inc(m_hi, 1)

            def router_and_silu(t):
                act.wait_ge(r_max, t + 1)
                act.activation(prob[:, t % 2, :], bank[:, 2 * (t % 2), 0:NE], ACT.Exp, bias=rneg[:, 0:1]).then_inc(r_exp, 1)
                if t >= 2:
                    act.wait_ge(m_act, t - 1)
                for c in range(2):
                    last = act.activation(sg[t % 2][:, c, :], bank[:, 2 * (t % 2) + c, (NE if c == 0 else 0):(NE if c == 0 else 0) + 384],
                                          ACT.Silu)
                last.then_inc(m_silu, 1)

            router_and_silu(0)
            for t in range(8):
                if t in (1, 3):
                    ln_high(14 + t // 2)
                if t < 7:
                    router_and_silu(t + 1)
                act.wait_ge(at_ready, t + 1)
                if t >= 2:
                    act.wait_ge(dn_ready, t - 1)
                act.activation(actT[t % 2][:].rearrange("p (a c) s -> p a (c s)", a=2),
                               bank[:, 2 * (t % 2):2 * (t % 2) + 2, 0:384], ACT.Copy).then_inc(at_out, 1)

        @block.vector
        def _(dve):
            step = [0]

            def mark(ins_):
                step[0] += 1
                ins_.then_inc(dve_step, 1)

            def sync():
                dve.wait_ge(dve_step, step[0])

            def ln_start(n):
                b, stage_ = n % 4, n // 4
                if stage_ == 0:
                    dve.wait_ge(ld_x[b], 16)
                elif stage_ < 3:
                    dve.wait_ge(x_done, n - 3)
                else:
                    dve.wait_ge(misc_done, MISC["O", b, 1] + 1)
                if n >= 1:
                    dve.wait_ge(ln_stats, n)
                for it in range(TT):
                    mark(dve.bn_stats(st6[:, it, :], X[:, 2 * b + it, :]))
                sync()
                for it in range(TT):
                    last = dve.bn_aggr(mv[:, n % 2, it, :], st6[:, it, :])
                last.then_inc(ln_stats, 1)

            def ln_finish(n):
                b = n % 4
                dve.wait_ge(ln_rstd, n + 1)
                if n >= 1:
                    dve.wait_ge(ln_T, n)
                for it in range(TT):
                    last = dve.tensor_scalar(XN[:, it, :], X[:, 2 * b + it, :], mv[:, n % 2, it, 0:1], rstd[:, n % 2, it:it + 1],
                                             ALU.subtract, ALU.mult)
                last.then_inc(ln_norm, 1)

            def ln_low(n):
                dve.wait_ge(ln_T, n + 1)
                dve.wait_ge(ln_hi, n + 1)
                dve.tensor_tensor(XL[:, n % 2, :, :], bank[:, 7, :].rearrange("p (t s) -> p t s", t=2),
                                  f32(XH[:, n % 2, :, :]), ALU.subtract).then_inc(misc_done, 1)

            ln_start(0)
            ln_start(1)
            for c in range(2):
                dve.wait_ge(kvT_hi, c + 1)
                dve.tensor_tensor(KTL[:, c * 512:(c + 1) * 512], bank[:, c, :], f32(KTH[:, c * 512:(c + 1) * 512]),
                                  ALU.subtract).then_inc(kvT_lo, 1)
            for c in range(2):
                dve.wait_ge(kv_hi, c + 1)
                dve.tensor_tensor(KVL[:, 4 * c:4 * c + 4, :], bank[:, 2 + c, :].rearrange("p (g d) -> p g d", g=4),
                                  f32(KVH[:, 4 * c:4 * c + 4, :]), ALU.subtract).then_inc(kv_lo, 1)
            ln_finish(0)
            ln_finish(1)
            ln_low(0)
            ln_low(1)
            def fold_step(i):
                if i >= 1:
                    dve.wait_ge(fM_hi, i)
                    dve.tensor_tensor(ML[:, :, (i - 1) * P:i * P], bank[:, 3, 0:2 * P].rearrange("p (t d) -> p t d", t=2),
                                      f32(MH[:, :, (i - 1) * P:i * P]), ALU.subtract).then_inc(fM_lo, 1)
                if i < NP:
                    dve.wait_ge(fE, i + 1)
                    if i >= 1:
                        dve.wait_ge(fM, i)
                    dve.tensor_copy(Esb[:, :], bank[:, 2, 0:D]).then_inc(fE_out, 1)

            def sim_update(b):
                dve.wait_ge(sim_exp, b + 1)
                mark(dve.reciprocal(rowrcp[:, b % 4, 0:TT], rowsum[:, b % 4, 0:TT]))
                sync()
                for it in range(TT):
                    last = dve.scalar_tensor_tensor(X[:, 2 * b + it, :], simn[:, it, :], rowrcp[:, b % 4, it:it + 1],
                                                    X[:, 2 * b + it, :], ALU.mult, ALU.add)
                last.then_inc(x_done, 1)

            def w_low(c):
                dve.wait_ge(w_hi, c + 1)
                dve.tensor_tensor(WL[:, c * 1024:(c + 1) * 1024], stage[:, c * 1024:(c + 1) * 1024],
                                  f32(WH[:, c * 1024:(c + 1) * 1024]), ALU.subtract).then_inc(w_lo, 1)

            for b in range(NB):
                dve.wait_ge(out_hi, b + 1)
                dve.tensor_tensor(outS[64:128, :], bank[64:128, 4, 0:S], f32(outS[64:128, :]), ALU.subtract).then_inc(out_lo, 1)
                ln_start(b + 2)
                if b >= 1:
                    sim_update(b - 1)
                fold_step(2 * b)
                ln_finish(b + 2)
                ln_low(b + 2)
                dve.wait_ge(sim_ready, b + 1)
                if b >= 1:
                    dve.wait_ge(sim_stats, b)
                simb = bank[:, 5, :].rearrange("p (t s) -> p t s", t=2)
                for it in range(TT):
                    mark(dve.bn_stats(st6s[:, it, :], simb[:, it, :]))
                sync()
                for it in range(TT):
                    last = dve.bn_aggr(mvs[:, b % 2, it, :], st6s[:, it, :])
                last.then_inc(sim_stats, 1)
                if b == 3:
                    w_low(0)
                    w_low(1)
                dve.wait_ge(sim_rstd, b + 1)
                for it in range(TT):
                    mark(dve.tensor_scalar(simn[:, it, :], simb[:, it, :], mvs[:, b % 2, it, 0:1], rstds[:, b % 2, it:it + 1],
                                           ALU.subtract, ALU.mult))
                if b == 0:
                    dve.wait_ge(ld_gb, 32)
                sync()
                mark(dve.tensor_tensor(simn[:], simn[:], gamma[:, :].unsqueeze(1).broadcast_to([P, TT, S]), ALU.mult))
                sync()
                mark(dve.tensor_tensor(simn[:], simn[:], beta[:, :].unsqueeze(1).broadcast_to([P, TT, S]), ALU.add))
                sync()
                dve.tensor_reduce(negmax[:, b % 4, 0:TT], simn[:], AX.X, ALU.max, negate=True).then_inc(sim_max, 1)
                fold_step(2 * b + 1)
            sim_update(NB - 1)
            w_low(2)
            w_low(3)
            fold_step(NP)
            ln_start(6)
            ln_finish(6)

            def add_x(b):
                dve.wait_ge(ffn_D, b + 1)
                dve.tensor_tensor(X[:, 2 * b:2 * b + 2, :], bank[:, 6, :].rearrange("p (t d) -> p t d", t=2),
                                  X[:, 2 * b:2 * b + 2, :], ALU.add).then_inc(x_done, 1)

            for u in range(8):
                h = hb[u % 4]
                dve.wait_ge(ffn_silu, u + 1)
                dve.wait_ge(ffn_U, u + 1)
                dve.tensor_tensor(h[:], bank[:, 4:6, :].rearrange("p a (k s) -> p (a k) s", k=2), h[:], ALU.mult).then_inc(ffn_h, 1)
                dve.wait_ge(ffn_abs, u + 1)
                pairs = ab[:].rearrange("p (a c) s -> p a c s", c=2)
                mark(dve.tensor_tensor(g1[:], pairs[:, :, 0, :], pairs[:, :, 1, :], ALU.is_ge))
                mark(dve.tensor_tensor(g2[:], ab[:, 0:2, :], ab[:, 2:4, :], ALU.is_ge))
                mark(dve.tensor_tensor(g3[:, 0, :], ab[:, 0, :], ab[:, 3, :], ALU.is_ge))
                dve.tensor_tensor(g3[:, 1, :], ab[:, 1, :], ab[:, 2, :], ALU.is_ge).then_inc(ffn_cmp, 1)
                dve.wait_ge(ffn_cmp, u + 1)
                sync()
                mark(dve.tensor_tensor(e2[:], g2[:], g3[:], ALU.add))
                mark(dve.tensor_tensor(f2[:, 0, :], g2[:, 0, :], g3[:, 1, :], ALU.add))
                mark(dve.tensor_tensor(f2[:, 1, :], g2[:, 1, :], g3[:, 0, :], ALU.add))
                sync()
                mark(dve.tensor_tensor(wins[:, 0, :], e2[:, 0, :], g1[:, 0, :], ALU.add))
                mark(dve.tensor_tensor(wins[:, 1, :], e2[:, 1, :], g1[:, 0, :], ALU.subtract))
                mark(dve.tensor_tensor(wins[:, 2, :], g1[:, 1, :], f2[:, 0, :], ALU.subtract))
                mark(dve.tensor_tensor(wins[:, 3, :], f2[:, 1, :], g1[:, 1, :], ALU.add))
                sync()
                for k, (at, op) in enumerate(((1.5, ALU.is_ge), (0.5, ALU.is_ge), (-0.5, ALU.is_ge), (1.5, ALU.is_le))):
                    last = dve.scalar_tensor_tensor(h[:, k, :], wins[:, k, :], at, h[:, k, :], op, ALU.mult)
                last.then_inc(ffn_hs, 1)
                if u % 2 == 1:
                    ln_low(6 + u // 2)
                    if u >= 3:
                        add_x(u // 2 - 1)
                    ln_start(7 + u // 2)
                    ln_finish(7 + u // 2)

            def q_low(b, pr):
                q = qS[b % 2]
                at = 7 if b else pr % 4
                dve.wait_ge(q_hi, 8 * b + pr + 1)
                dve.tensor_tensor(q[64:128, 2 * pr, :], bank[0:64, at, 0:S], f32(q[0:64, 2 * pr, :]), ALU.subtract)
                dve.tensor_tensor(q[0:64, 2 * pr + 1, :], bank[64:128, at, 0:S], f32(q[64:128, 2 * pr + 1, :]),
                                  ALU.subtract).then_inc(misc_done if b else q0_low, 1)

            def add_o(b, it):
                dve.wait_ge(o_ready, 2 * b + it + 1)
                dve.tensor_tensor(X[:, 2 * b + it, :], bank[:, 7, 0:D], X[:, 2 * b + it, :], ALU.add).then_inc(misc_done, 1)

            for pr in range(4):
                q_low(0, pr)
            add_x(3)
            for pr in range(4, NP):
                q_low(0, pr)
            ln_low(10)
            for g in range(NG):
                mark(dve.tensor_scalar(onehot[:, g, :], mg[:, :], float(g), None, ALU.is_equal))
            for u in range(STEPS):
                if 2 <= u <= UNITS + 1:
                    v = u - 2
                    dve.wait_ge(pt_ready, 2 * v + 1)
                    if v // 2 >= 2:
                        dve.wait_ge(pv_ready, v // 2 - 1)
                    dve.tensor_copy(PT[v // 2 % 2][:, 0, :, (v % 2) * P:(v % 2 + 1) * P],
                                    bank[:, 4, :].rearrange("p (h s) -> p h s", h=4)).then_inc(pt_out0, 1)
                if 1 <= u <= UNITS:
                    v = u - 1
                    dve.wait_ge(p_exp, v + 1)
                    dve.reciprocal(rowrcp[:, v % 4, :], rowsum[:, v % 4, :]).then_inc(p_rcp, 1)
                if u < UNITS:
                    dve.wait_ge(sc_ready, u + 1)
                    dve.tensor_reduce(negmax[:, u % 4, :],
                                      bank[:, 2 * (u % 2):2 * (u % 2) + 2, :].rearrange("p a (h s) -> p (a h) s", h=2),
                                      AX.X, ALU.max, negate=True).then_inc(sc_max, 1)
                if u % 8 in (5, 6) and u > 8:
                    add_o(u // 8 - 1, u % 8 - 5)
                if u < 24:
                    q_low(u // 8 + 1, u % 8)
                if u in (8, 16, 24):
                    ln_low(10 + u // 8)
                if u >= 4 and u % 2 == 0 and u <= UNITS + 2:
                    w = (u - 4) // 2
                    b, quad = w // 4, w % 4
                    dve.wait_ge(pv_ready, w + 1)
                    if b >= 2:
                        dve.wait_ge(o_ready, 2 * (b - 1))
                    dve.tensor_copy(ctxT[b % 2][:, 2 * quad:2 * quad + 2, :],
                                    bank[:, 6, :].rearrange("p (c s) -> p c s", c=2)).then_inc(ctx_out, 1)
                if u in (6, 14, 22, 30):
                    ln_start(11 + u // 8)
                if u in (7, 15, 23, 31):
                    ln_finish(11 + u // 8)
                if u in (5, 6, 7, 8):
                    c = u - 5
                    t, a = c // 2, (c % 2) * (WM // 2)
                    dve.wait_ge(m_hi, c + 1)
                    dve.tensor_tensor(WLm[:, t, a:a + WM // 2], stageM[:, t, a:a + WM // 2],
                                      f32(WHm[:, t, a:a + WM // 2]), ALU.subtract).then_inc(m_lo, 1)
            add_o(3, 1)

            def router(t):
                logits = bank[:, 2 * (t % 2), 0:NE]
                dve.wait_ge(g_ready, t + 1)
                mark(dve.max(mx8[:, :], logits))
                sync()
                dve.tensor_scalar(rneg[:, :], mx8[:, 0:1], -1.0, None, ALU.mult).then_inc(r_max, 1)
                dve.wait_ge(r_exp, t + 1)
                pr_ = prob[:, t % 2, :]
                mark(dve.max(top8[:, :], pr_))
                sync()
                mark(dve.match_replace(left[:, :], top8[:, :], pr_, -1.0))
                mark(dve.tensor_reduce(tsum[:, :], top8[:, :], AX.X, ALU.add))
                sync()
                mark(dve.scalar_tensor_tensor(psel[:, :], left[:, :], 0.0, pr_, ALU.is_lt, ALU.mult))
                mark(dve.reciprocal(trcp[:, :], tsum[:, :]))
                sync()
                mark(dve.tensor_tensor(pgrp[:], onehot[:], psel[:, :].unsqueeze(1).broadcast_to([P, NG, NE]), ALU.mult))
                sync()
                mark(dve.tensor_reduce(wsum[:, :], pgrp[:], AX.X, ALU.add))
                sync()
                mark(dve.tensor_scalar(wtg[:, :], wsum[:, :], trcp[:, 0:1], None, ALU.mult))
                sync()

            def weighted(t):
                dve.wait_ge(u_ready, t + 1)
                dve.wait_ge(m_silu, t + 1)
                if t >= 2:
                    dve.wait_ge(at_ready, t - 1)
                for g in range(NG):
                    last = dve.scalar_tensor_tensor(actb[t % 2][:, g * EI:(g + 1) * EI],
                                                    bank[:, 4 + g // 4, (g % 4) * EI:(g % 4 + 1) * EI], wtg[:, g:g + 1],
                                                    sg[t % 2][:, g // 4, (g % 4) * EI:(g % 4 + 1) * EI], ALU.mult, ALU.mult)
                last.then_inc(m_act, 1)

            def finish(t):
                dve.wait_ge(dn_ready, t + 1)
                dve.tensor_tensor(X[:, t, :], bank[:, 6, 0:D], X[:, t, :], ALU.add).then_inc(x_out, 1)

            ln_start(15)
            router(0)
            for t in range(8):
                weighted(t)
                if t in (1, 3):
                    ln_low(14 + t // 2)
                if t == 2:
                    ln_finish(15)
                if t < 7:
                    router(t + 1)
                if t >= 1:
                    finish(t - 1)
            finish(7)

        @block.tensor
        def _(pe):
            def three(dst, pairs):
                n = 0
                for sh, sl, mh, ml in pairs:
                    for a, m in ((sh, mh), (sl, mh), (sh, ml)):
                        last = pe.matmul(dst, a, m, start=(n == 0), stop=(n == 3 * len(pairs) - 1))
                        n += 1
                return last

            def misc_free(use):
                if MISC[use] > 0:
                    pe.wait_ge(misc_done, MISC[use])

            def misc_emptied(*use):
                pe.wait_ge(misc_done, MISC[use] + 1)

            def ln_transpose(n):
                pe.wait_ge(ln_norm, n + 1)
                misc_free(("T", n))
                for it in range(TT):
                    for t in range(2):
                        last = pe.transpose(bank[:, 7, t * S + it * P:t * S + (it + 1) * P], XN[:, it, t * P:(t + 1) * P], ident[:, :])
                last.then_inc(ln_T, 1)

            pe.wait_ge(ld_kv, 32)
            for c in range(2):
                pe.matmul(bank[:, c, :], WkA[0:65, :], ctxA[0:65, c * 512:(c + 1) * 512], start=True, stop=True).then_inc(kvT_ready, 1)
            for g in range(NB * TT):
                last = pe.matmul(bank[:, 2 + g // 4, (g % 4) * P:(g % 4 + 1) * P], ctxA[0:65, g * P:(g + 1) * P], WkA[0:65, :],
                                 start=True, stop=True)
                if g % 4 == 3:
                    last.then_inc(kv_ready, 1)
            pe.wait_ge(ld_id, 16)
            ln_transpose(0)
            ln_transpose(1)
            def fold(i):
                if i < NP:
                    if i % 2 == 0:
                        pe.wait_ge(ld_fold[i // 2], 96)
                    for c in range(2):
                        h = 2 * i + c
                        if i >= 1:
                            pe.wait_ge(fD_out, h - 1)
                        for j in range(2):
                            last = pe.matmul(bank[0:96, c, j * D:(j + 1) * D], kcq[:, h, j * 96:(j + 1) * 96], wq[:, h, :],
                                             start=True, stop=True)
                        last.then_inc(fD, 1)
                    if i >= 1:
                        pe.wait_ge(fN_out, i)
                    for c in range(2):
                        last = pe.matmul(bank[64 * c:64 * c + 64, 6, 0:D], kckv[:, 2 * i + c, :], woT[:, 2 * i + c, :],
                                         start=True, stop=True)
                    last.then_inc(fN, 1)
                if i >= 1:
                    pe.wait_ge(fE_out, i)
                    if i >= 2:
                        pe.wait_ge(fM_lo, i - 1)
                    for t in range(2):
                        last = pe.matmul(bank[:, 3, t * P:(t + 1) * P], Esb[:, t * P:(t + 1) * P], krB[:, i - 1, :],
                                         start=True, stop=True)
                    last.then_inc(fM, 1)
                if i < NP:
                    pe.wait_ge(fD_out, 2 * i + 2)
                    if i >= 1:
                        pe.wait_ge(fE_out, i)
                    for j in range(2):
                        for c in range(2):
                            last = pe.matmul(bank[64 * c:64 * c + 64, 2, 0:D], qr[0:96, j, 2 * i + c, :], lat[0:96, c, j, :],
                                             start=(j == 0), stop=(j == 1))
                    last.then_inc(fE, 1)

            pe.wait_ge(kv_lo, 2)
            pe.wait_ge(kvT_lo, 2)
            for b in range(NB):
                slot = b % 2
                misc_emptied("T", b)
                if b >= 1:
                    pe.wait_ge(out_lo, b)
                three(bank[:, 4, 0:S], [(KVH[:, 2 * b + j, :], KVL[:, 2 * b + j, :], XH[:, slot, j, :], XL[:, slot, j, :])
                                        for j in range(2)]).then_inc(out_ready, 1)
                fold(2 * b)
                ln_transpose(b + 2)
                pe.wait_ge(out_lo, b + 1)
                if b >= 1:
                    pe.wait_ge(sim_max, b)
                for it in range(TT):
                    for n, k in enumerate((KTH, KTL)):
                        last = pe.matmul(bank[:, 5, it * S:(it + 1) * S], outS[:, it * P:(it + 1) * P],
                                         k[:, b * S:(b + 1) * S], start=(n == 0), stop=(n == 1))
                last.then_inc(sim_ready, 1)
                fold(2 * b + 1)
            fold(NP)

            def gate_up(u):
                b, mh = u // 2, u % 2
                slot = b % 2
                if mh == 0:
                    misc_emptied("T", 4 + b)
                if u == 0:
                    pe.wait_ge(w_lo, 4)
                    pe.wait_ge(fM_lo, NP)
                    pe.wait_ge(fE_out, NP)
                if u >= 2:
                    pe.wait_ge(ffn_silu, u - 1)
                for s in range(2):
                    if s == 1:
                        if u == 0:
                            pe.wait_ge(x_done, 4)
                        else:
                            pe.wait_ge(ffn_h, u)
                    for k in range(4):
                        at = 2 * (u % 2) + k // 2 if s == 0 else 4 + k // 2
                        last = three(bank[:, at, (k % 2) * S:(k % 2 + 1) * S],
                                     [(WHf[:, t, s, k, mh * P:(mh + 1) * P], WLf[:, t, s, k, mh * P:(mh + 1) * P],
                                       XH[:, slot, t, :], XL[:, slot, t, :]) for t in range(2)])
                    last.then_inc(ffn_U if s else ffn_G, 1)

            def down(b):
                pe.wait_ge(ffn_hs, 2 * b + 2)
                pe.wait_ge(x_done, 4 + b)
                if b == 0:
                    pe.wait_ge(ld_wd, 16)
                    pe.wait_ge(fN_out, NP)
                for it in range(TT):
                    for j in range(8):
                        last = pe.matmul(bank[:, 6, it * D:(it + 1) * D], hb[(2 * b + j // 4) % 4][:, j % 4, it * P:(it + 1) * P],
                                         wd[:, j, :], start=(j == 0), stop=(j == 7))
                last.then_inc(ffn_D, 1)

            for u in range(8):
                gate_up(u)
                if u % 2 == 1:
                    ln_transpose(6 + u // 2)
                    if u >= 3:
                        down(u // 2 - 1)

            def queries(b, pr):
                if pr == 0:
                    misc_emptied("T", 8 + b)
                if b:
                    misc_free(("Q", b, pr))
                elif pr == 0:
                    pe.wait_ge(ffn_silu, 8)
                elif pr >= 4:
                    pe.wait_ge(q0_low, pr - 3)
                cols = slice(pr * P, (pr + 1) * P)
                three(bank[:, 7 if b else pr % 4, 0:S], [(MH[:, t, cols], ML[:, t, cols], XH[:, b % 2, t, :], XL[:, b % 2, t, :])
                                        for t in range(2)]).then_inc(q_ready, 1)

            def scores(u):
                b, quad, it = u // 8, u % 8 // 2, u % 2
                if b:
                    misc_emptied("Q", b, 2 * quad + 1)
                elif u < 2:
                    pe.wait_ge(q0_low, NP)
                if u == 0:
                    pe.wait_ge(rope_done, 1)
                if u >= 2:
                    pe.wait_ge(p_exp, u - 1)
                for h in range(4):
                    for n, k in enumerate((KRH, KRL)):
                        last = pe.matmul(bank[:, 2 * (u % 2) + h // 2, (h % 2) * S:(h % 2 + 1) * S],
                                         qS[b % 2][:, 4 * quad + h, it * P:(it + 1) * P], k[:, b * S:(b + 1) * S],
                                         start=(n == 0), stop=(n == 1))
                last.then_inc(sc_ready, 1)

            def probs_transpose(u):
                pe.wait_ge(p_norm, u + 1)
                for lt in range(2):
                    if u >= 1:
                        pe.wait_ge(pt_out1 if lt else pt_out0, u)
                    for h in range(4):
                        last = pe.transpose(bank[:, 4 + lt, h * P:(h + 1) * P], Pb[u % 2][:, h, lt * P:(lt + 1) * P], ident[:, :])
                    last.then_inc(pt_ready, 1)

            def context(w):
                b = w // 4
                pe.wait_ge(pt_out0, 2 * w + 2)
                pe.wait_ge(pt_out1, 2 * w + 2)
                if w == 0:
                    pe.wait_ge(x_done, 8)
                else:
                    pe.wait_ge(ctx_out, w)
                for c in range(2):
                    for lt in range(2):
                        for j in range(2):
                            last = pe.matmul(bank[64 * j:64 * j + 64, 6, c * S:(c + 1) * S], KVN[:, 2 * b + lt, :],
                                             PT[w % 2][:, lt, 2 * c + j, :], start=(lt == 0), stop=(lt == 1))
                last.then_inc(pv_ready, 1)

            def attn_out(b, it):
                pe.wait_ge(ctx_out, 4 * b + 4)
                misc_free(("O", b, it))
                for pr in range(NP):
                    last = pe.matmul(bank[:, 7, 0:D], ctxT[b % 2][:, pr, it * P:(it + 1) * P], NN[:, pr, :],
                                     start=(pr == 0), stop=(pr == NP - 1))
                last.then_inc(o_ready, 1)

            def moe(t, half_):
                b, it = t // 2, t % 2
                edges = (0, 416, 800, 1184, WM)
                for c in range(2 * half_, 2 * half_ + 2):
                    at = (2 * (t % 2) if half_ == 0 else 4) + c % 2
                    a, z = edges[c], edges[c + 1]
                    last = three(bank[:, at, 0:z - a],
                                 [(XH[:, b % 2, k, it * P:(it + 1) * P], XL[:, b % 2, k, it * P:(it + 1) * P],
                                   WHm[:, k, a:z], WLm[:, k, a:z]) for k in range(2)])
                last.then_inc(u_ready if half_ else g_ready, 1)

            def moe_gate(t):
                if t == 0:
                    pe.wait_ge(m_lo, 4)
                    pe.wait_ge(p_exp, UNITS - 1)
                if t % 2 == 0:
                    misc_emptied("T", 12 + t // 2)
                if t >= 2:
                    pe.wait_ge(at_out, t - 1)
                moe(t, 0)

            def moe_up(t):
                if t == 0:
                    pe.wait_ge(pt_out0, 32)
                    pe.wait_ge(pt_out1, 32)
                else:
                    pe.wait_ge(m_act, t)
                moe(t, 1)

            def act_transpose(t):
                pe.wait_ge(m_act, t + 1)
                for c in range(6):
                    last = pe.transpose(bank[:, 2 * (t % 2) + c // 3, (c % 3) * P:(c % 3 + 1) * P],
                                        actb[t % 2][:, c * P:(c + 1) * P], ident[:, :])
                last.then_inc(at_ready, 1)

            def moe_down(t):
                pe.wait_ge(at_out, t + 1)
                if t == 0:
                    pe.wait_ge(ld_dn, 16 * N_DN)
                    pe.wait_ge(ctx_out, 16)
                else:
                    pe.wait_ge(x_out, t)
                for c in range(6):
                    last = pe.matmul(bank[:, 6, 0:D], actT[t % 2][:, c, :], dnT[:, c, :], start=(c == 0), stop=(c == 5))
                last.then_inc(dn_ready, 1)

            for pr in range(4):
                queries(0, pr)
            down(3)
            for pr in range(4, NP):
                queries(0, pr)
            ln_transpose(10)
            for u in range(STEPS):
                if 2 <= u <= UNITS + 1:
                    probs_transpose(u - 2)
                if u < UNITS:
                    scores(u)
                if u < 24:
                    queries(u // 8 + 1, u % 8)
                if u in (8, 16, 24):
                    ln_transpose(10 + u // 8)
                if u == UNITS + 1:
                    moe_gate(0)
                if u % 2 == 0 and 4 <= u <= UNITS + 2:
                    context((u - 4) // 2)
                if u == UNITS + 3:
                    moe_up(0)
                if u % 8 in (4, 5) and u > 8:
                    attn_out(u // 8 - 1, u % 8 - 4)
            for t in range(8):
                if t:
                    moe_up(t)
                if t in (1, 3):
                    ln_transpose(14 + t // 2)
                if t < 7:
                    moe_gate(t + 1)
                act_transpose(t)
                if t >= 1:
                    moe_down(t - 1)
            moe_down(7)


def layout(i):
    c = np.ascontiguousarray
    x, ctx = i["x"], i["ctx_512"]
    f = x.dtype
    ctxT = ctx.transpose(2, 0, 1).reshape(DC, NB * S)
    ctxA = np.concatenate([ctxT, np.ones((1, NB * S), f)])
    WkA = np.concatenate([i["L0_xattn_W_k"].T, i["L0_xattn_b_k"][None, :]])
    gu = np.stack([i["L0_ffn_w_gate"], i["L0_ffn_w_up"]])
    gu = gu.reshape(2, 2, P, S, 4).transpose(2, 1, 0, 4, 3)
    wd = i["L0_ffn_w_down"].reshape(2, P, 4, D).transpose(1, 0, 2, 3)
    kr = i["L1_xattn_W_kr"]
    krB = np.zeros((P, NP, P), f)
    for j in range(2):
        krB[64 * j:64 * j + 64, :, 64 * j:64 * j + 64] = kr[j::2].transpose(2, 0, 1)
    gup = i["L1_ffn_gate_up_proj"].reshape(NE, 2, EI, 2, P).transpose(0, 1, 4, 3, 2)
    inv = (np.float32(1.0) / np.float32(10000.0) ** (np.arange(0, DC, 2, dtype=np.float32) / np.float32(DC))).astype(np.float32)
    freq = np.arange(S, dtype=np.float32)[:, None] * inv[None, :]
    sin, cos = (np.repeat(g(freq), 2, axis=-1).astype(np.float32) for g in (np.sin, np.cos))
    sin = np.where(np.arange(DC) < DC // 2, -sin, sin).astype(np.float32)
    kN = ctx.reshape(NB * TT, P, DC).transpose(1, 0, 2)
    out = {
        "x": x, "ctxA": ctxA, "WkA": np.concatenate([WkA, WkA], axis=1), "ident": np.eye(P, dtype=np.float32),
        "gamma": i["L0_xattn_ln_gamma"], "beta": i["L0_xattn_ln_beta"],
        "wq": i["L1_xattn_Wq"].reshape(NH, HK, D).transpose(1, 0, 2),
        "kcq": i["L1_xattn_w_kc_q"].transpose(1, 0, 2),
        "qr": i["L1_xattn_W_qr"].reshape(NH, 2, 96, DC).transpose(2, 1, 0, 3),
        "krB": krB, "kckv": i["L1_xattn_w_kc_kv"].transpose(1, 0, 2),
        "woT": i["L1_xattn_Wo"].reshape(D, NH, HK).transpose(2, 1, 0),
        "wgu": gu.reshape(P, 4 * FFN), "wd": wd.reshape(P, 8, D),
        "kT": np.concatenate([ctxT, ctxT]), "kTrot": np.concatenate([np.roll(ctxT, 32, 0)] * 2),
        "cosT": np.concatenate([cos.T, cos.T]), "sinT": np.concatenate([sin.T, sin.T]),
        "kN": kN, "kNrot": np.roll(kN, 32, 2),
        "cosN": cos.reshape(TT, P, DC).transpose(1, 0, 2), "sinN": sin.reshape(TT, P, DC).transpose(1, 0, 2),
        "dom": i["L1_ffn_dominant_experts"].reshape(1, NG), "mg": i["L1_ffn_merge_groups"],
        "gwT": i["L1_ffn_gate_weight"].reshape(NE, 2, P).transpose(2, 1, 0),
        "gup": gup, "dn": i["L1_ffn_down_proj"].transpose(0, 2, 1),
    }
    return {k: c(v) for k, v in out.items()}


def kernel(**inputs):
    import concourse.bacc as bacc
    from concourse.bass_utils import run_bass_kernel_spmd

    arrays = layout({k: np.asarray(v) for k, v in inputs.items()})
    nc = bacc.Bacc("TRN2", target_bir_lowering=False, num_devices=1)
    ins = {k: nc.dram_tensor(f"in_{k}", v.shape, mybir.dt.from_np(v.dtype), kind="ExternalInput").ap()
           for k, v in arrays.items()}
    out = nc.dram_tensor("out_x", (NB, S, D), F32, kind="ExternalOutput").ap()
    two_layers(nc, ins, out)
    r = run_bass_kernel_spmd(nc, [{f"in_{k}": v for k, v in arrays.items()}], core_ids=[0])
    return r.results[0]["out_x"]
```

```python
from contextlib import ExitStack

import numpy as np

import concourse.bass as bass
from concourse import mybir

P = 128
NB = 4
S = 256
TT = 2
D = 256
DC = 64
FFN = 1024
NH = 16
HK = 128
DQ = 192
NP = NH // 2
NE = 32
NG = 8
EI = 96
GC = NG * EI
WM = NE + 2 * GC
UNITS = NB * 8
STEPS = UNITS + 6
LN_STEPS = {5: 10, 9: 11, 17: 12, 25: 13}
M_STEPS = (11, 13, 19, 21)
LN_STARTS = {3: 10, 7: 11, 15: 12, 23: 13, 31: 14}
Q0_BANKS = (0, 2, 4, 5)
OUT_STEPS = {11: [(0, 0)], 13: [(0, 1)], 19: [(1, 0)], 21: [(1, 1)], 27: [(2, 0)], 29: [(2, 1)],
             35: [(3, 0), (3, 1)]}
LN_EPS = 1e-5
W_ORDER = (0, 2, 1, 3)
SIM_EPS = 1e-6 * D

ALU = mybir.AluOpType
ACT = mybir.ActivationFunctionType
AX = mybir.AxisListType
F32 = mybir.dt.float32
F32R = mybir.dt.float32r
BF16 = mybir.dt.bfloat16
I32 = mybir.dt.int32


def two_layers(nc, ins, out):
    with ExitStack() as ctx:
        def sb(name, shape, dt=F32, stack=ctx):
            return stack.enter_context(nc.sbuf_tensor(name, shape, dt))

        def sem(name):
            return ctx.enter_context(nc.semaphore(name))

        def overlay(*sets):
            def size(spec):
                n = 2 if spec[2] == BF16 else 4
                for k in spec[1][1:]:
                    n *= k
                return n
            most = max(sum(map(size, s)) for s in sets)
            tiles = {}
            for i, s in enumerate(sets):
                stack = ExitStack() if i < len(sets) - 1 else ctx
                for spec in s:
                    tiles[spec[0]] = sb(*spec, stack=stack)
                if stack is not ctx:
                    stack.close()
                elif (pad := most - sum(map(size, s))) > 0:
                    sb(f"pad_{s[0][0]}", [P, pad // 4], F32)
            return tiles

        X = sb("X", [P, NB * TT, D])
        XN = sb("XN", [P, TT, D])
        XH = sb("XH", [P, 2, 2, S], F32R)
        XL = sb("XL", [P, 2, 2, S], F32R)
        WH = sb("WH", [P, 2 * 2 * FFN], F32R)
        WL = sb("WL", [P, 2 * 2 * FFN], F32R)
        MH = sb("MH", [P, 2, NH * DC], F32R)
        ML = sb("ML", [P, 2, NH * DC], F32R)
        NN = sb("NN", [P, NP, D])
        KRH = sb("KRH", [P, NB * S], F32R)
        KRL = sb("KRL", [P, NB * S], F32R)
        KVN = sb("KVN", [P, NB * TT, DC])
        ident = sb("ident", [P, P])
        st6 = sb("st6", [P, TT, 6])
        st6s = sb("st6s", [P, TT, 6])
        mv = sb("mv", [P, 2, TT, 2])
        mvs = sb("mvs", [P, 2, TT, 2])
        var_eps = sb("var_eps", [P, TT])
        rstd = sb("rstd", [P, 2, TT])
        rstds = sb("rstds", [P, 2, TT])
        half = sb("half", [P, TT])
        negmax = sb("negmax", [P, 4, 4])
        rowsum = sb("rowsum", [P, 4, 4])
        rowrcp = sb("rowrcp", [P, 4, 4])
        dom = sb("dom", [1, NG], I32)
        mg = sb("mg", [P, NE], I32)

        r1 = overlay([("wq", [P, NH, D], F32), ("kcq", [P, NH, DQ], F32), ("qr", [P, 2, NH, DC], F32)],
                     [("qS0", [P, NH, S], F32R), ("qS1", [P, NH, S], F32R)])
        r2 = overlay([("woT", [P, NH, D], F32)],
                     [("ctx0", [P, NP, S], F32), ("ctx1", [P, NP, S], F32)])
        r3 = overlay([("ctxA", [P, NB * S], F32), ("KTH", [P, NB * S], F32R), ("KTL", [P, NB * S], F32R),
                      ("KVH", [P, NB * TT, P], F32R), ("KVL", [P, NB * TT, P], F32R),
                      ("lat", [P, 2, 2, D], F32)],
                     [("kT", [P, NB * S], F32), ("kTrot", [P, NB * S], F32), ("cosT", [P, S], F32),
                      ("sinT", [P, S], F32), ("kN", [P, NB * TT, DC], F32), ("kNrot", [P, NB * TT, DC], F32),
                      ("cosN", [P, TT, DC], F32), ("sinN", [P, TT, DC], F32)],
                     [("P0", [P, 4, S], F32), ("P1", [P, 4, S], F32),
                      ("PT0", [P, 2, 4, S], F32), ("PT1", [P, 2, 4, S], F32)])
        r4 = overlay([("stage", [P, 2 * 2 * FFN], F32), ("Esb", [P, D], F32)],
                     [("hb0", [P, 4, S], F32), ("hb1", [P, 4, S], F32), ("hb2", [P, 4, S], F32),
                      ("hb3", [P, 4, S], F32), ("ab", [P, 4, S], F32), ("g1", [P, 2, S], BF16),
                      ("g2", [P, 2, S], BF16), ("g3", [P, 2, S], BF16), ("e2", [P, 2, S], BF16),
                      ("f2", [P, 2, S], BF16), ("wins", [P, 4, S], BF16)],
                     [("stageM", [P, 2, WM], F32), ("sg0", [P, 2, 384], F32), ("sg1", [P, 2, 384], F32),
                      ("act0", [P, GC], F32), ("act1", [P, GC], F32),
                      ("actT0", [P, 6, P], F32), ("actT1", [P, 6, P], F32)])
        r5 = overlay([("krB", [P, NP, P], F32), ("kckv", [P, NH, DC], F32)],
                     [("wd", [P, 8, D], F32)],
                     [("dnT", [P, 6, D], F32)])
        r6 = overlay([("simn", [P, TT, S], F32), ("gamma", [P, S], F32), ("beta", [P, S], F32), ("outS", [P, S], F32R)],
                     [("onehot", [P, NG, NE], F32), ("pgrp", [P, NG, NE], F32),
                      ("prob", [P, 2, NE], F32), ("left", [P, NE], F32), ("psel", [P, NE], F32)])
        WkA = sb("WkA", [P, P])
        mx8 = sb("mx8", [P, 8])
        rneg = sb("rneg", [P, 1])
        top8 = sb("top8", [P, 8])
        wsum = sb("wsum", [P, NG])
        tsum = sb("tsum", [P, 1])
        trcp = sb("trcp", [P, 1])
        wtg = sb("wtg", [P, NG])

        simn, gamma, beta, outS = (r6[k] for k in ("simn", "gamma", "beta", "outS"))
        onehot, pgrp, prob, left, psel = (r6[k] for k in ("onehot", "pgrp", "prob", "left", "psel"))
        wq, kcq, qr = r1["wq"], r1["kcq"], r1["qr"]
        qS = [r1["qS0"], r1["qS1"]]
        woT, ctxT = r2["woT"], [r2["ctx0"], r2["ctx1"]]
        ctxA, KTH, KTL, KVH, KVL, lat = (r3[k] for k in ("ctxA", "KTH", "KTL", "KVH", "KVL", "lat"))
        Pb, PT = [r3["P0"], r3["P1"]], [r3["PT0"], r3["PT1"]]
        stage = r4["stage"]
        kT, kTrot, cosT, sinT, kN, kNrot, cosN, sinN = (
            r3[k] for k in ("kT", "kTrot", "cosT", "sinT", "kN", "kNrot", "cosN", "sinN"))
        Esb = r4["Esb"]
        hb = [r4[f"hb{i}"] for i in range(4)]
        ab, g1, g2, g3, e2, f2, wins = (r4[k] for k in ("ab", "g1", "g2", "g3", "e2", "f2", "wins"))
        stageM, sg, actb, actT = r4["stageM"], [r4["sg0"], r4["sg1"]], [r4["act0"], r4["act1"]], [r4["actT0"], r4["actT1"]]
        krB, kckv, wd, dnT = r5["krB"], r5["kckv"], r5["wd"], r5["dnT"]

        bank = ctx.enter_context(nc.psum_tensor("bank", [P, 8, 512], F32))

        ld_x = [sem(f"ld_x{b}") for b in range(NB)]
        ld_kv, ld_gb, ld_rope, ld_wgu, ld_wd, ld_moe, ld_dn, ld_idx, ld_id = (
            sem(f"ld_{k}") for k in ("kv", "gb", "rope", "wgu", "wd", "moe", "dn", "idx", "id"))
        ld_fold = [sem(f"ld_fold{c}") for c in range(4)]
        stored = sem("stored")
        dve_step, pool_step = sem("dve_step"), sem("pool_step")
        ln_stats, ln_rstd, ln_norm, ln_T, ln_hi = (sem(k) for k in ("ln_stats", "ln_rstd", "ln_norm", "ln_T", "ln_hi"))
        ln_lo = sem("ln_lo")
        x_done = sem("x_done")
        kvT_ready, kvT_hi, kvT_lo, kv_ready, kv_hi, kv_lo = (
            sem(k) for k in ("kvT_ready", "kvT_hi", "kvT_lo", "kv_ready", "kv_hi", "kv_lo"))
        out_ready, out_hi, out_lo, sim_ready, sim_stats, sim_rstd, sim_max, sim_exp = (
            sem(k) for k in ("out_ready", "out_hi", "out_lo", "sim_ready", "sim_stats", "sim_rstd", "sim_max", "sim_exp"))
        fD, fD_out, fE, fE_out, fM, fM_hi, fM_lo, fN, fN_out = (
            sem(k) for k in ("fD", "fD_out", "fE", "fE_out", "fM", "fM_hi", "fM_lo", "fN", "fN_out"))
        w_hi, w_lo, ffn_G, ffn_U, ffn_silu, ffn_h, ffn_abs, ffn_cmp, ffn_hs, ffn_D = (
            sem(k) for k in ("w_hi", "w_lo", "ffn_G", "ffn_U", "ffn_silu", "ffn_h", "ffn_abs", "ffn_cmp", "ffn_hs", "ffn_D"))
        q_ready, q_hi, sc_ready, sc_max, p_exp, p_rcp, p_norm, pt_ready, pt_out0, pt_out1, pv_ready, ctx_out, o_ready, o_out, q_lo, rope_done = (
            sem(k) for k in ("q_ready", "q_hi", "sc_ready", "sc_max", "p_exp", "p_rcp", "p_norm", "pt_ready",
                             "pt_out0", "pt_out1", "pv_ready", "ctx_out", "o_ready", "o_out", "q_lo", "rope_done"))
        m_hi, m_lo, g_ready, u_ready, r_max, r_exp, m_silu, m_act, at_ready, at_out, dn_ready, x_out = (
            sem(k) for k in ("m_hi", "m_lo", "g_ready", "u_ready", "r_max", "r_exp", "m_silu", "m_act",
                             "at_ready", "at_out", "dn_ready", "x_out"))

        WHm = WH[:, 0:2 * WM].rearrange("p (t c) -> p t c", t=2)
        WLm = WL[:, 0:2 * WM].rearrange("p (t c) -> p t c", t=2)
        WHf = WH[:, :].rearrange("p (t s k m) -> p t s k m", t=2, s=2, k=4)
        WLf = WL[:, :].rearrange("p (t s k m) -> p t s k m", t=2, s=2, k=4)

        def f32(ap):
            return ap.bitcast(F32)

        def xin_done(eng, n):
            b = n % 4
            for stage_, s_, count in ((0, out_ready, b + 1), (1, ffn_U, 4 * b + 4), (2, q_ready, 4 * b + 4),
                                      (3, u_ready, 2 * b + 2)):
                if n // 4 == stage_:
                    eng.wait_ge(s_, count)

        def ln_bank(n):
            return 6 if n in LN_STEPS.values() else 7

        def out_bank(b, it):
            return 7 if (b, it) == (NB - 1, 1) else 6

        block = ctx.enter_context(nc.Block())

        @block.sync
        def _(sp):
            sp.dma_start(ctxA[0:65, :], ins["ctxA"]).then_inc(ld_kv, 16)
            sp.dma_start(WkA[0:65, :], ins["WkA"]).then_inc(ld_kv, 16)
            sp.dma_start(ident[:, :], ins["ident"]).then_inc(ld_id, 16)
            for b in range(NB):
                sp.dma_start(X[:, 2 * b:2 * b + 2, :], ins["x"][b].rearrange("(t p) d -> p t d", p=P)).then_inc(ld_x[b], 16)
            sp.dma_start(gamma[:, :], ins["gamma"].partition_broadcast(P)).then_inc(ld_gb, 16)
            sp.dma_start(beta[:, :], ins["beta"].partition_broadcast(P)).then_inc(ld_gb, 16)
            for c in range(4):
                hs = slice(4 * c, 4 * c + 4)
                for tile, name in ((kcq, "kcq"), (wq, "wq"), (kckv, "kckv"), (woT, "woT")):
                    sp.dma_start(tile[:, hs], ins[name][:, hs]).then_inc(ld_fold[c], 16)
                sp.dma_start(qr[0:96, :, hs], ins["qr"][:, :, hs]).then_inc(ld_fold[c], 16)
                sp.dma_start(krB[:, 2 * c:2 * c + 2], ins["krB"][:, 2 * c:2 * c + 2]).then_inc(ld_fold[c], 16)
            sp.dma_start(stage[:], ins["wgu"]).then_inc(ld_wgu, 16)
            sp.dma_start(dom[:, :], ins["dom"]).then_inc(ld_idx, 16)
            sp.dma_start(mg[:, :], ins["mg"].partition_broadcast(P)).then_inc(ld_idx, 16)
            sp.wait_ge(fM, NP)
            sp.wait_ge(fN, NP)
            sp.dma_start(wd[:], ins["wd"]).then_inc(ld_wd, 16)
            for tile, name in ((kT, "kT"), (kTrot, "kTrot"), (cosT, "cosT"), (sinT, "sinT"), (kN, "kN"),
                               (kNrot, "kNrot"), (cosN, "cosN"), (sinN, "sinN")):
                sp.dma_start(tile[:], ins[name]).then_inc(ld_rope, 16)
            sp.wait_ge(ld_idx, 32)
            expert = [sp.value_load(dom[0:1, g:g + 1], min_val=0, max_val=NE - 1) for g in range(NG)]
            sp.wait_ge(x_done, 8)
            for t in range(2):
                sp.dma_start(stageM[:, t, 0:NE], ins["gwT"][:, t, :]).then_inc(ld_moe, 16)
            for g in range(NG):
                for s in range(2):
                    at = NE + s * GC + g * EI
                    sp.dma_start(stageM[:, :, at:at + EI],
                                 ins["gup"][bass.ds(expert[g], 1), s].rearrange("a p t c -> p (a t) c")).then_inc(ld_moe, 16)
            for g in range(NG):
                done = 0
                while done < EI:
                    row = g * EI + done
                    k = min(EI - done, P - row % P)
                    sp.dma_start(dnT[row % P:row % P + k, row // P, :],
                                 ins["dn"][bass.ds(expert[g], 1), done:done + k].rearrange("a i d -> (a i) d")).then_inc(ld_dn, 16)
                    done += k
            for t in range(NB * TT):
                sp.wait_ge(x_out, t + 1)
                sp.dma_start(out[t // 2, (t % 2) * P:(t % 2 + 1) * P, :], X[:, t, :]).then_inc(stored, 16)
            sp.wait_ge(stored, 16 * NB * TT)

        N_DN = sum(len({(g * EI) // P, (g * EI + EI - 1) // P}) for g in range(NG))

        @block.gpsimd
        def _(pool):
            step = [0]

            def link(ins_):
                step[0] += 1
                ins_.then_inc(pool_step, 1)
                pool.wait_ge(pool_step, step[0])

            link(pool.memset(half[:], -0.5))

            def ln(n):
                pool.wait_ge(ln_stats, n + 1)
                link(pool.tensor_scalar(var_eps[:], mv[:, n % 2, :, 1], LN_EPS, 1.0, ALU.add, ALU.mult))
                pool.tensor_tensor(rstd[:, n % 2, :], var_eps[:], half[:], ALU.pow).then_inc(ln_rstd, 1)
                pool.wait_ge(ln_rstd, n + 1)

            def sim(b):
                pool.wait_ge(sim_stats, b + 1)
                link(pool.tensor_scalar(var_eps[:], mvs[:, b % 2, :, 1], SIM_EPS, 1.0, ALU.add, ALU.mult))
                pool.tensor_tensor(rstds[:, b % 2, :], var_eps[:], half[:], ALU.pow).then_inc(sim_rstd, 1)
                pool.wait_ge(sim_rstd, b + 1)

            ln(0)
            ln(1)
            def w_low(i):
                pool.wait_ge(w_hi, i + 1)
                c = slice(W_ORDER[i] * FFN, (W_ORDER[i] + 1) * FFN)
                pool.tensor_tensor(WL[:, c], stage[:, c], f32(WH[:, c]), ALU.subtract).then_inc(w_lo, 1)

            for b in range(NB):
                ln(b + 2)
                if b == 3:
                    w_low(3)
                sim(b)
                if b == 1:
                    w_low(0)
                if b == 2:
                    w_low(1)
                    w_low(2)
            ln(6)
            pool.wait_ge(ld_rope, 16 * 8)
            kT4 = kT[:].rearrange("p (b l) -> p b l", b=NB)
            kTrot4 = kTrot[:].rearrange("p (b l) -> p b l", b=NB)
            kN4 = kN[:].rearrange("p (b t) d -> p b t d", b=NB)
            kNrot4 = kNrot[:].rearrange("p (b t) d -> p b t d", b=NB)
            for t in range(TT):
                for tab, dst in ((cosN, kN4), (sinN, kNrot4)):
                    link(pool.tensor_tensor(dst[:, :, t, :], dst[:, :, t, :],
                                            tab[:, t, :].unsqueeze(1).broadcast_to([P, NB, DC]), ALU.mult))
            link(pool.tensor_tensor(KVN[:], kN[:], kNrot[:], ALU.add))
            link(pool.tensor_tensor(kT4, kT4, cosT[:, :].unsqueeze(1).broadcast_to([P, NB, S]), ALU.mult))
            link(pool.tensor_tensor(kTrot4, kTrot4, sinT[:, :].unsqueeze(1).broadcast_to([P, NB, S]), ALU.mult))
            ln(7)
            link(pool.tensor_tensor(kT[:], kT[:], kTrot[:], ALU.add))
            link(pool.tensor_copy(KRH[:], kT[:]))
            pool.tensor_tensor(KRL[:], kT[:], f32(KRH[:]), ALU.subtract).then_inc(rope_done, 1)
            for n in range(8, 10):
                ln(n)

            def scale(u):
                pool.wait_ge(p_rcp, u + 1)
                for h in range(4):
                    last = pool.tensor_scalar(Pb[u % 2][:, h, :], Pb[u % 2][:, h, :], rowrcp[:, u % 4, h:h + 1], 1.0,
                                              ALU.mult, ALU.mult)
                last.then_inc(p_norm, 1)

            for u in range(STEPS):
                if 1 <= u <= UNITS:
                    scale(u - 1)
                if u in LN_STARTS:
                    ln(LN_STARTS[u])
            ln(15)

        @block.scalar
        def _(act):
            def ln_high(n):
                act.wait_ge(ln_T, n + 1)
                if n >= 2:
                    xin_done(act, n - 2)
                act.activation(XH[:, n % 2, :, :], bank[:, ln_bank(n), :].rearrange("p (t s) -> p t s", t=2),
                               ACT.Copy).then_inc(ln_hi, 1)

            def kvT_high(c):
                act.wait_ge(kvT_ready, c + 1)
                act.activation(KTH[:, c * 512:(c + 1) * 512], bank[:, c, :], ACT.Copy).then_inc(kvT_hi, 1)

            def kv_high(c):
                act.wait_ge(kv_ready, c + 1)
                act.activation(KVH[:, 4 * c:4 * c + 4, :], bank[:, 2 + c, :].rearrange("p (g d) -> p g d", g=4),
                               ACT.Copy).then_inc(kv_hi, 1)

            kvT_high(0)
            kv_high(0)
            ln_high(0)
            kv_high(1)
            kvT_high(1)

            def fold_out(i):
                if i < NP:
                    for c in range(2):
                        act.wait_ge(fD, 2 * i + c + 1)
                        if i >= 1:
                            act.wait_ge(fE, i)
                        act.activation(lat[0:96, c, :, :], bank[0:96, c, :].rearrange("p (j d) -> p j d", j=2),
                                       ACT.Copy).then_inc(fD_out, 1)
                    act.wait_ge(fN, i + 1)
                    act.activation(NN[:, i, :], bank[:, 6, 0:D], ACT.Copy).then_inc(fN_out, 1)
                if i >= 1:
                    act.wait_ge(fM, i)
                    act.activation(MH[:, :, (i - 1) * P:i * P], bank[:, 3, 0:2 * P].rearrange("p (t d) -> p t d", t=2),
                                   ACT.Copy).then_inc(fM_hi, 1)

            def sim_softmax(b):
                act.wait_ge(sim_max, b + 1)
                for it in range(TT):
                    last = act.activation(simn[:, it, :], simn[:, it, :], ACT.Exp, bias=negmax[:, b % 4, it:it + 1],
                                          accum_out=rowsum[:, b % 4, it:it + 1])
                last.then_inc(sim_exp, 1)

            def w_high(i):
                if i == 0:
                    act.wait_ge(ld_wgu, 16)
                c = slice(W_ORDER[i] * FFN, (W_ORDER[i] + 1) * FFN)
                act.activation(WH[:, c], stage[:, c],
                               ACT.Copy).then_inc(w_hi, 1)

            for b in range(NB):
                act.wait_ge(out_ready, b + 1)
                if b >= 1:
                    act.wait_ge(sim_ready, b)
                act.activation(outS[:, :], bank[:, 4, 0:S], ACT.Copy).then_inc(out_hi, 1)
                if b == 0:
                    ln_high(1)
                if b >= 1:
                    sim_softmax(b - 1)
                fold_out(2 * b)
                fold_out(2 * b + 1)
                ln_high(b + 2)
                if b == 1:
                    w_high(0)
                    w_high(1)
                if b == 2:
                    w_high(2)
                    w_high(3)
            sim_softmax(NB - 1)
            fold_out(NP)

            for u in range(8):
                b = u // 2
                act.wait_ge(ffn_G, u + 1)
                if b >= 2:
                    act.wait_ge(ffn_D, b - 1)
                act.activation(hb[u % 4][:], bank[:, 2 * (u % 2):2 * (u % 2) + 2, :].rearrange("p a (k s) -> p (a k) s", k=2),
                               ACT.Silu).then_inc(ffn_silu, 1)
                if u >= 1:
                    act.wait_ge(ffn_cmp, u)
                for c in range(2):
                    act.wait_ge(ffn_h, 2 * u + c + 1)
                    act.activation(ab[:, 2 * c:2 * c + 2, :], hb[u % 4][:, 2 * c:2 * c + 2, :], ACT.Abs).then_inc(ffn_abs, 1)
                if u % 2 == 1:
                    ln_high(6 + u // 2)

            def q_high(b, c):
                act.wait_ge(q_ready, 4 * b + c + 1)
                if b >= 2:
                    act.wait_ge(sc_ready, 8 * (b - 1))
                for j in range(2):
                    rows = slice(64 * j, 64 * j + 64)
                    last = act.activation(qS[b % 2][rows, 4 * c + j:4 * c + 4:2, :],
                                          bank[rows, 7 if b else Q0_BANKS[c], :].rearrange("p (k s) -> p k s", k=2), ACT.Copy)
                last.then_inc(q_hi, 1)

            def router_and_silu(t):
                act.wait_ge(r_max, t + 1)
                act.activation(prob[:, t % 2, :], bank[:, 2 * (t % 2), 0:NE], ACT.Exp, bias=rneg[:, 0:1]).then_inc(r_exp, 1)
                if t >= 2:
                    act.wait_ge(m_act, t - 1)
                for c in range(2):
                    last = act.activation(sg[t % 2][:, c, :], bank[:, 2 * (t % 2) + c, (NE if c == 0 else 0):(NE if c == 0 else 0) + 384],
                                          ACT.Silu)
                last.then_inc(m_silu, 1)

            for c in range(4):
                q_high(0, c)
            for u in range(STEPS):
                if 2 <= u <= UNITS + 1:
                    v = u - 2
                    act.wait_ge(pt_ready, 2 * v + 2)
                    if v // 2 >= 2:
                        act.wait_ge(pv_ready, v // 2 - 1)
                    act.activation(PT[v // 2 % 2][:, 1, :, (v % 2) * P:(v % 2 + 1) * P],
                                   bank[:, 5, :].rearrange("p (h s) -> p h s", h=4), ACT.Copy).then_inc(pt_out1, 1)
                if u in LN_STEPS:
                    ln_high(LN_STEPS[u])
                if u < UNITS:
                    act.wait_ge(sc_max, u + 1)
                    for h in range(4):
                        last = act.activation(Pb[u % 2][:, h, :], bank[:, 2 * (u % 2) + h // 2, (h % 2) * S:(h % 2 + 1) * S],
                                              ACT.Exp, bias=negmax[:, u % 4, h:h + 1], accum_out=rowsum[:, u % 4, h:h + 1])
                    last.then_inc(p_exp, 1)
                if u < 24 and u % 2 == 1:
                    q_high(u // 8 + 1, u % 8 // 2)
                if u == UNITS + 1:
                    router_and_silu(0)
                if u in M_STEPS:
                    c = M_STEPS.index(u)
                    if c == 0:
                        act.wait_ge(ld_moe, 16 * 18)
                    t, a = c // 2, (c % 2) * (WM // 2)
                    act.activation(WHm[:, t, a:a + WM // 2], stageM[:, t, a:a + WM // 2], ACT.Copy).then_inc(m_hi, 1)

            for t in range(8):
                if t in (2, 4):
                    ln_high(13 + t // 2)
                if t < 7:
                    router_and_silu(t + 1)
                act.wait_ge(at_ready, t + 1)
                if t >= 2:
                    act.wait_ge(dn_ready, t - 1)
                act.activation(actT[t % 2][:].rearrange("p (a c) s -> p a (c s)", a=2),
                               bank[:, 2 * (t % 2):2 * (t % 2) + 2, 0:384], ACT.Copy).then_inc(at_out, 1)

        @block.vector
        def _(dve):
            step = [0]

            def mark(ins_):
                step[0] += 1
                ins_.then_inc(dve_step, 1)

            def sync():
                dve.wait_ge(dve_step, step[0])

            def ln_start(n):
                b, stage_ = n % 4, n // 4
                if stage_ == 0:
                    dve.wait_ge(ld_x[b], 16)
                elif stage_ < 3:
                    dve.wait_ge(x_done, n - 3)
                else:
                    dve.wait_ge(o_out, 2 * b + 2)
                if n >= 1:
                    dve.wait_ge(ln_stats, n)
                for it in range(TT):
                    mark(dve.bn_stats(st6[:, it, :], X[:, 2 * b + it, :]))
                sync()
                for it in range(TT):
                    last = dve.bn_aggr(mv[:, n % 2, it, :], st6[:, it, :])
                last.then_inc(ln_stats, 1)

            def ln_finish(n):
                b = n % 4
                dve.wait_ge(ln_rstd, n + 1)
                if n >= 1:
                    dve.wait_ge(ln_T, n)
                for it in range(TT):
                    last = dve.tensor_scalar(XN[:, it, :], X[:, 2 * b + it, :], mv[:, n % 2, it, 0:1], rstd[:, n % 2, it:it + 1],
                                             ALU.subtract, ALU.mult)
                last.then_inc(ln_norm, 1)

            def ln_low(n):
                dve.wait_ge(ln_T, n + 1)
                dve.wait_ge(ln_hi, n + 1)
                dve.tensor_tensor(XL[:, n % 2, :, :], bank[:, ln_bank(n), :].rearrange("p (t s) -> p t s", t=2),
                                  f32(XH[:, n % 2, :, :]), ALU.subtract).then_inc(ln_lo, 1)

            def kvT_low(c):
                dve.wait_ge(kvT_hi, c + 1)
                dve.tensor_tensor(KTL[:, c * 512:(c + 1) * 512], bank[:, c, :], f32(KTH[:, c * 512:(c + 1) * 512]),
                                  ALU.subtract).then_inc(kvT_lo, 1)

            def kv_low(c):
                dve.wait_ge(kv_hi, c + 1)
                dve.tensor_tensor(KVL[:, 4 * c:4 * c + 4, :], bank[:, 2 + c, :].rearrange("p (g d) -> p g d", g=4),
                                  f32(KVH[:, 4 * c:4 * c + 4, :]), ALU.subtract).then_inc(kv_lo, 1)

            ln_start(0)
            kvT_low(0)
            ln_finish(0)
            kv_low(0)
            ln_start(1)
            ln_low(0)
            kv_low(1)
            ln_finish(1)
            kvT_low(1)

            def fold_step(i):
                if i >= 1:
                    dve.wait_ge(fM_hi, i)
                    dve.tensor_tensor(ML[:, :, (i - 1) * P:i * P], bank[:, 3, 0:2 * P].rearrange("p (t d) -> p t d", t=2),
                                      f32(MH[:, :, (i - 1) * P:i * P]), ALU.subtract).then_inc(fM_lo, 1)
                if i < NP:
                    dve.wait_ge(fE, i + 1)
                    if i >= 1:
                        dve.wait_ge(fM, i)
                    dve.tensor_copy(Esb[:, :], bank[:, 2, 0:D]).then_inc(fE_out, 1)

            def sim_update(b):
                dve.wait_ge(sim_exp, b + 1)
                mark(dve.reciprocal(rowrcp[:, b % 4, 0:TT], rowsum[:, b % 4, 0:TT]))
                sync()
                for it in range(TT):
                    last = dve.scalar_tensor_tensor(X[:, 2 * b + it, :], simn[:, it, :], rowrcp[:, b % 4, it:it + 1],
                                                    X[:, 2 * b + it, :], ALU.mult, ALU.add)
                last.then_inc(x_done, 1)

            for b in range(NB):
                dve.wait_ge(out_hi, b + 1)
                dve.tensor_tensor(outS[64:128, :], bank[64:128, 4, 0:S], f32(outS[64:128, :]), ALU.subtract).then_inc(out_lo, 1)
                if b == 0:
                    ln_low(1)
                ln_start(b + 2)
                if b >= 1:
                    sim_update(b - 1)
                fold_step(2 * b)
                ln_finish(b + 2)
                dve.wait_ge(sim_ready, b + 1)
                if b >= 1:
                    dve.wait_ge(sim_stats, b)
                simb = bank[:, 5, :].rearrange("p (t s) -> p t s", t=2)
                for it in range(TT):
                    mark(dve.bn_stats(st6s[:, it, :], simb[:, it, :]))
                sync()
                for it in range(TT):
                    last = dve.bn_aggr(mvs[:, b % 2, it, :], st6s[:, it, :])
                last.then_inc(sim_stats, 1)
                if b == 0:
                    dve.wait_ge(ld_gb, 32)
                dve.wait_ge(sim_stats, b + 1)
                for it in range(TT):
                    mark(dve.scalar_tensor_tensor(simn[:, it, :], simb[:, it, :], mvs[:, b % 2, it, 0:1], gamma[:, :],
                                                  ALU.subtract, ALU.mult))
                fold_step(2 * b + 1)
                dve.wait_ge(sim_rstd, b + 1)
                sync()
                for it in range(TT):
                    mark(dve.scalar_tensor_tensor(simn[:, it, :], simn[:, it, :], rstds[:, b % 2, it:it + 1], beta[:, :],
                                                  ALU.mult, ALU.add))
                sync()
                dve.tensor_reduce(negmax[:, b % 4, 0:TT], simn[:], AX.X, ALU.max, negate=True).then_inc(sim_max, 1)
                ln_low(b + 2)
            fold_step(NP)
            sim_update(NB - 1)
            ln_start(6)
            ln_finish(6)

            def add_x(b):
                dve.wait_ge(ffn_D, b + 1)
                dve.tensor_tensor(X[:, 2 * b:2 * b + 2, :], bank[:, 6, :].rearrange("p (t d) -> p t d", t=2),
                                  X[:, 2 * b:2 * b + 2, :], ALU.add).then_inc(x_done, 1)

            def between(b):
                ln_low(6 + b)
                ln_start(7 + b)
                ln_finish(7 + b)

            for u in range(8):
                h = hb[u % 4]
                if u % 2 == 0 and u >= 4:
                    add_x(u // 2 - 2)
                dve.wait_ge(ffn_silu, u + 1)
                for c in range(2):
                    dve.wait_ge(ffn_U, 2 * u + c + 1)
                    dve.tensor_tensor(h[:, 2 * c:2 * c + 2, :], bank[:, 4 + c, :].rearrange("p (k s) -> p k s", k=2),
                                      h[:, 2 * c:2 * c + 2, :], ALU.mult).then_inc(ffn_h, 1)
                if u % 2 == 0 and u >= 2:
                    between(u // 2 - 1)
                dve.wait_ge(ffn_abs, 2 * u + 2)
                pairs = ab[:].rearrange("p (a c) s -> p a c s", c=2)
                mark(dve.tensor_tensor(g1[:], pairs[:, :, 0, :], pairs[:, :, 1, :], ALU.is_ge))
                mark(dve.tensor_tensor(g2[:], ab[:, 0:2, :], ab[:, 2:4, :], ALU.is_ge))
                mark(dve.tensor_tensor(g3[:, 0, :], ab[:, 0, :], ab[:, 3, :], ALU.is_ge))
                dve.tensor_tensor(g3[:, 1, :], ab[:, 1, :], ab[:, 2, :], ALU.is_ge).then_inc(ffn_cmp, 1)
                dve.wait_ge(ffn_cmp, u + 1)
                sync()
                mark(dve.tensor_tensor(e2[:], g2[:], g3[:], ALU.add))
                mark(dve.tensor_tensor(f2[:, 0, :], g2[:, 0, :], g3[:, 1, :], ALU.add))
                mark(dve.tensor_tensor(f2[:, 1, :], g2[:, 1, :], g3[:, 0, :], ALU.add))
                sync()
                mark(dve.tensor_tensor(wins[:, 0, :], e2[:, 0, :], g1[:, 0, :], ALU.add))
                mark(dve.tensor_tensor(wins[:, 1, :], e2[:, 1, :], g1[:, 0, :], ALU.subtract))
                mark(dve.tensor_tensor(wins[:, 2, :], g1[:, 1, :], f2[:, 0, :], ALU.subtract))
                mark(dve.tensor_tensor(wins[:, 3, :], f2[:, 1, :], g1[:, 1, :], ALU.add))
                sync()
                for k, (at, op) in enumerate(((1.5, ALU.is_ge), (0.5, ALU.is_ge), (-0.5, ALU.is_ge), (1.5, ALU.is_le))):
                    last = dve.scalar_tensor_tensor(h[:, k, :], wins[:, k, :], at, h[:, k, :], op, ALU.mult)
                last.then_inc(ffn_hs, 1)
            add_x(2)

            def q_low(b, c):
                q = qS[b % 2]
                dve.wait_ge(q_hi, 4 * b + c + 1)
                for j in range(2):
                    rows, other = slice(64 * j, 64 * j + 64), slice(64 - 64 * j, 128 - 64 * j)
                    last = dve.tensor_tensor(q[other, 4 * c + j:4 * c + 4:2, :],
                                             bank[rows, 7 if b else Q0_BANKS[c], :].rearrange("p (k s) -> p k s", k=2),
                                             f32(q[rows, 4 * c + j:4 * c + 4:2, :]), ALU.subtract)
                last.then_inc(q_lo, 1)

            def router(t):
                logits = bank[:, 2 * (t % 2), 0:NE]
                dve.wait_ge(g_ready, t + 1)
                mark(dve.max(mx8[:, :], logits))
                sync()
                dve.tensor_scalar(rneg[:, :], mx8[:, 0:1], -1.0, None, ALU.mult).then_inc(r_max, 1)
                dve.wait_ge(r_exp, t + 1)
                pr_ = prob[:, t % 2, :]
                mark(dve.max(top8[:, :], pr_))
                sync()
                mark(dve.match_replace(left[:, :], top8[:, :], pr_, -1.0))
                mark(dve.tensor_reduce(tsum[:, :], top8[:, :], AX.X, ALU.add))
                sync()
                mark(dve.scalar_tensor_tensor(psel[:, :], left[:, :], 0.0, pr_, ALU.is_lt, ALU.mult))
                mark(dve.reciprocal(trcp[:, :], tsum[:, :]))
                sync()
                mark(dve.tensor_tensor(pgrp[:], onehot[:], psel[:, :].unsqueeze(1).broadcast_to([P, NG, NE]), ALU.mult))
                sync()
                mark(dve.tensor_reduce(wsum[:, :], pgrp[:], AX.X, ALU.add))
                sync()
                mark(dve.tensor_scalar(wtg[:, :], wsum[:, :], trcp[:, 0:1], None, ALU.mult))
                sync()

            def add_o(b, it):
                dve.wait_ge(o_ready, 2 * b + it + 1)
                dve.tensor_tensor(X[:, 2 * b + it, :], bank[:, out_bank(b, it), 0:D], X[:, 2 * b + it, :], ALU.add).then_inc(o_out, 1)

            for c in range(3):
                q_low(0, c)
            for u in range(STEPS):
                if 2 <= u <= UNITS + 1:
                    v = u - 2
                    dve.wait_ge(pt_ready, 2 * v + 1)
                    if v // 2 >= 2:
                        dve.wait_ge(pv_ready, v // 2 - 1)
                    dve.tensor_copy(PT[v // 2 % 2][:, 0, :, (v % 2) * P:(v % 2 + 1) * P],
                                    bank[:, 4, :].rearrange("p (h s) -> p h s", h=4)).then_inc(pt_out0, 1)
                if 1 <= u <= UNITS:
                    v = u - 1
                    dve.wait_ge(p_exp, v + 1)
                    dve.reciprocal(rowrcp[:, v % 4, :], rowsum[:, v % 4, :]).then_inc(p_rcp, 1)
                if u - 1 in OUT_STEPS and u < UNITS:
                    add_o(*OUT_STEPS[u - 1][0])
                if u < UNITS:
                    dve.wait_ge(sc_ready, u + 1)
                    dve.tensor_reduce(negmax[:, u % 4, :],
                                      bank[:, 2 * (u % 2):2 * (u % 2) + 2, :].rearrange("p a (h s) -> p (a h) s", h=2),
                                      AX.X, ALU.max, negate=True).then_inc(sc_max, 1)
                if u in LN_STEPS:
                    ln_low(LN_STEPS[u])
                if u == 0:
                    q_low(0, 3)
                    ln_low(9)
                if u == 1:
                    add_x(3)
                    for g in range(NG):
                        mark(dve.tensor_scalar(onehot[:, g, :], mg[:, :], float(g), None, ALU.is_equal))
                if u - 1 in LN_STARTS:
                    ln_finish(LN_STARTS[u - 1])
                if 2 <= u <= 24 and u % 2 == 0:
                    q_low((u - 1) // 8 + 1, (u - 1) % 8 // 2)
                if u >= 4 and u % 2 == 0 and u <= UNITS + 2:
                    w = (u - 4) // 2
                    b, quad = w // 4, w % 4
                    dve.wait_ge(pv_ready, w + 1)
                    if b >= 2:
                        dve.wait_ge(o_ready, 2 * (b - 1))
                    dve.tensor_copy(ctxT[b % 2][:, 2 * quad:2 * quad + 2, :],
                                    bank[:, 6, :].rearrange("p (c s) -> p c s", c=2)).then_inc(ctx_out, 1)
                if u == UNITS + 1:
                    router(0)
                if u in LN_STARTS:
                    ln_start(LN_STARTS[u])
                if u in M_STEPS:
                    c = M_STEPS.index(u)
                    t, a = c // 2, (c % 2) * (WM // 2)
                    dve.wait_ge(m_hi, c + 1)
                    dve.tensor_tensor(WLm[:, t, a:a + WM // 2], stageM[:, t, a:a + WM // 2],
                                      f32(WHm[:, t, a:a + WM // 2]), ALU.subtract).then_inc(m_lo, 1)
            def weighted(t):
                dve.wait_ge(u_ready, t + 1)
                dve.wait_ge(m_silu, t + 1)
                if t >= 2:
                    dve.wait_ge(at_ready, t - 1)
                for g in range(NG):
                    last = dve.scalar_tensor_tensor(actb[t % 2][:, g * EI:(g + 1) * EI],
                                                    bank[:, 4 + g // 4, (g % 4) * EI:(g % 4 + 1) * EI], wtg[:, g:g + 1],
                                                    sg[t % 2][:, g // 4, (g % 4) * EI:(g % 4 + 1) * EI], ALU.mult, ALU.mult)
                last.then_inc(m_act, 1)

            weighted(0)
            add_o(3, 0)
            router(1)
            add_o(3, 1)

            def finish(t):
                dve.wait_ge(dn_ready, t + 1)
                dve.tensor_tensor(X[:, t, :], bank[:, 6, 0:D], X[:, t, :], ALU.add).then_inc(x_out, 1)

            ln_start(15)
            for t in range(8):
                if t:
                    weighted(t)
                if t in (2, 4):
                    ln_low(13 + t // 2)
                if t == 3:
                    ln_finish(15)
                if 1 <= t < 7:
                    router(t + 1)
                if t >= 1:
                    finish(t - 1)
            finish(7)

        @block.tensor
        def _(pe):
            def three(dst, pairs):
                n = 0
                for sh, sl, mh, ml in pairs:
                    for a, m in ((sh, mh), (sl, mh), (sh, ml)):
                        last = pe.matmul(dst, a, m, start=(n == 0), stop=(n == 3 * len(pairs) - 1))
                        n += 1
                return last

            def ln_transpose(n):
                pe.wait_ge(ln_norm, n + 1)
                if n in LN_STEPS.values():
                    pe.wait_ge(ctx_out, next(u for u in LN_STEPS if LN_STEPS[u] == n) // 2 - 1)
                elif n == 14:
                    pe.wait_ge(o_out, 2 * NB)
                elif n >= 1:
                    pe.wait_ge(ln_lo, n)
                for it in range(TT):
                    for t in range(2):
                        last = pe.transpose(bank[:, ln_bank(n), t * S + it * P:t * S + (it + 1) * P], XN[:, it, t * P:(t + 1) * P], ident[:, :])
                last.then_inc(ln_T, 1)

            def kvT_product(c):
                pe.matmul(bank[:, c, :], WkA[0:65, :], ctxA[0:65, c * 512:(c + 1) * 512], start=True, stop=True).then_inc(kvT_ready, 1)

            def kv_product(c):
                for g in range(4 * c, 4 * c + 4):
                    last = pe.matmul(bank[:, 2 + c, (g % 4) * P:(g % 4 + 1) * P], ctxA[0:65, g * P:(g + 1) * P], WkA[0:65, :],
                                     start=True, stop=True)
                last.then_inc(kv_ready, 1)

            pe.wait_ge(ld_kv, 32)
            kvT_product(0)
            kv_product(0)
            pe.wait_ge(ld_id, 16)
            ln_transpose(0)
            kv_product(1)
            kvT_product(1)

            def fold(i):
                if i < NP:
                    if i % 2 == 0:
                        pe.wait_ge(ld_fold[i // 2], 96)
                    for c in range(2):
                        h = 2 * i + c
                        if i >= 1:
                            pe.wait_ge(fD_out, h - 1)
                        for j in range(2):
                            last = pe.matmul(bank[0:96, c, j * D:(j + 1) * D], kcq[:, h, j * 96:(j + 1) * 96], wq[:, h, :],
                                             start=True, stop=True)
                        last.then_inc(fD, 1)
                    if i >= 1:
                        pe.wait_ge(fN_out, i)
                    for c in range(2):
                        last = pe.matmul(bank[64 * c:64 * c + 64, 6, 0:D], kckv[:, 2 * i + c, :], woT[:, 2 * i + c, :],
                                         start=True, stop=True)
                    last.then_inc(fN, 1)
                if i >= 1:
                    pe.wait_ge(fE_out, i)
                    if i >= 2:
                        pe.wait_ge(fM_lo, i - 1)
                    for t in range(2):
                        last = pe.matmul(bank[:, 3, t * P:(t + 1) * P], Esb[:, t * P:(t + 1) * P], krB[:, i - 1, :],
                                         start=True, stop=True)
                    last.then_inc(fM, 1)
                if i < NP:
                    pe.wait_ge(fD_out, 2 * i + 2)
                    if i >= 1:
                        pe.wait_ge(fE_out, i)
                    for j in range(2):
                        for c in range(2):
                            last = pe.matmul(bank[64 * c:64 * c + 64, 2, 0:D], qr[0:96, j, 2 * i + c, :], lat[0:96, c, j, :],
                                             start=(j == 0), stop=(j == 1))
                    last.then_inc(fE, 1)

            for b in range(NB):
                slot = b % 2
                pe.wait_ge(ln_lo, b + 1)
                pe.wait_ge(kv_lo, b // 2 + 1)
                if b >= 1:
                    pe.wait_ge(out_lo, b)
                three(bank[:, 4, 0:S], [(KVH[:, 2 * b + j, :], KVL[:, 2 * b + j, :], XH[:, slot, j, :], XL[:, slot, j, :])
                                        for j in range(2)]).then_inc(out_ready, 1)
                if b == 0:
                    ln_transpose(1)
                    pe.wait_ge(kv_lo, 2)
                    pe.wait_ge(kvT_lo, 2)
                fold(2 * b)
                pe.wait_ge(out_lo, b + 1)
                if b >= 1:
                    pe.wait_ge(sim_max, b)
                for it in range(TT):
                    for n, k in enumerate((KTH, KTL)):
                        last = pe.matmul(bank[:, 5, it * S:(it + 1) * S], outS[:, it * P:(it + 1) * P],
                                         k[:, b * S:(b + 1) * S], start=(n == 0), stop=(n == 1))
                last.then_inc(sim_ready, 1)
                fold(2 * b + 1)
                ln_transpose(b + 2)

            def ffn(u, s, k, dst):
                b, mh = u // 2, u % 2
                return three(bank[:, dst + k // 2, (k % 2) * S:(k % 2 + 1) * S],
                             [(WHf[:, t, s, k, mh * P:(mh + 1) * P], WLf[:, t, s, k, mh * P:(mh + 1) * P],
                               XH[:, b % 2, t, :], XL[:, b % 2, t, :]) for t in range(2)])

            def gate(u):
                if u % 2 == 0:
                    pe.wait_ge(ln_lo, 5 + u // 2)
                if u == 0:
                    pe.wait_ge(w_lo, 2)
                    pe.wait_ge(fD_out, NH)
                elif u == 1:
                    pe.wait_ge(fM_lo, NP)
                    pe.wait_ge(fE_out, NP)
                else:
                    pe.wait_ge(ffn_silu, u - 1)
                for k in range(4):
                    last = ffn(u, 0, k, 2 * (u % 2))
                last.then_inc(ffn_G, 1)

            def up(u):
                if u == 0:
                    pe.wait_ge(w_lo, 4)
                    pe.wait_ge(x_done, 4)
                for k in range(4):
                    if u and k % 2 == 0:
                        pe.wait_ge(ffn_h, 2 * u - 1 + k // 2)
                    last = ffn(u, 1, k, 4)
                    if k % 2 == 1:
                        last.then_inc(ffn_U, 1)

            def down(b, it):
                if it == 0:
                    pe.wait_ge(ffn_hs, 2 * b + 2)
                    pe.wait_ge(x_done, 4 + b)
                if b == 0 and it == 0:
                    pe.wait_ge(ld_wd, 16)
                    pe.wait_ge(fN_out, NP)
                for j in range(8):
                    last = pe.matmul(bank[:, 6, it * D:(it + 1) * D], hb[(2 * b + j // 4) % 4][:, j % 4, it * P:(it + 1) * P],
                                     wd[:, j, :], start=(j == 0), stop=(j == 7))
                if it == 1:
                    last.then_inc(ffn_D, 1)

            gate(0)
            fold(NP)
            for u in range(8):
                if u % 2 == 0:
                    if u < 7:
                        gate(u + 1)
                    up(u)
                    if u >= 2:
                        down(u // 2 - 1, 0)
                else:
                    up(u)
                    ln_transpose(6 + u // 2)
                    if u < 7:
                        gate(u + 1)
                    if u >= 3:
                        down(u // 2 - 1, 1)

            def queries(b, c):
                if c == 0:
                    pe.wait_ge(ln_lo, 9 + b)
                if b == 0 and c < 2:
                    pe.wait_ge(ffn_silu, 7 + c)
                elif b == 0:
                    pe.wait_ge(ffn_h, 16)
                else:
                    pe.wait_ge(q_lo, 4 * b + c)
                for k in range(2):
                    cols = slice((2 * c + k) * P, (2 * c + k + 1) * P)
                    last = three(bank[:, 7 if b else Q0_BANKS[c], k * S:(k + 1) * S],
                                 [(MH[:, t, cols], ML[:, t, cols], XH[:, b % 2, t, :], XL[:, b % 2, t, :])
                                  for t in range(2)])
                last.then_inc(q_ready, 1)

            def scores(u):
                b, quad, it = u // 8, u % 8 // 2, u % 2
                pe.wait_ge(q_lo, u + 1 if u < 2 else 4 * b + quad + 1)
                if u < 2:
                    pe.wait_ge(ffn_silu, 7 + u)
                if u == 0:
                    pe.wait_ge(rope_done, 1)
                if u >= 2:
                    pe.wait_ge(p_exp, u - 1)
                for h in range(4):
                    for n, k in enumerate((KRH, KRL)):
                        last = pe.matmul(bank[:, 2 * (u % 2) + h // 2, (h % 2) * S:(h % 2 + 1) * S],
                                         qS[b % 2][:, 4 * quad + h, it * P:(it + 1) * P], k[:, b * S:(b + 1) * S],
                                         start=(n == 0), stop=(n == 1))
                last.then_inc(sc_ready, 1)

            def probs_transpose(u):
                pe.wait_ge(p_norm, u + 1)
                if u == 0:
                    pe.wait_ge(q_lo, 4)
                for lt in range(2):
                    if u >= 1:
                        pe.wait_ge(pt_out1 if lt else pt_out0, u)
                    for h in range(4):
                        last = pe.transpose(bank[:, 4 + lt, h * P:(h + 1) * P], Pb[u % 2][:, h, lt * P:(lt + 1) * P], ident[:, :])
                    last.then_inc(pt_ready, 1)

            def context(w):
                b = w // 4
                pe.wait_ge(pt_out0, 2 * w + 2)
                pe.wait_ge(pt_out1, 2 * w + 2)
                if w == 0:
                    pe.wait_ge(x_done, 8)
                else:
                    pe.wait_ge(ctx_out, w)
                if (n := LN_STEPS.get(2 * w + 3)) is not None:
                    pe.wait_ge(ln_lo, n + 1)
                for o in OUT_STEPS.get(2 * w + 3, []):
                    pe.wait_ge(o_out, 2 * o[0] + o[1] + 1)
                for c in range(2):
                    for lt in range(2):
                        for j in range(2):
                            last = pe.matmul(bank[64 * j:64 * j + 64, 6, c * S:(c + 1) * S], KVN[:, 2 * b + lt, :],
                                             PT[w % 2][:, lt, 2 * c + j, :], start=(lt == 0), stop=(lt == 1))
                last.then_inc(pv_ready, 1)

            def attn_out(b, it):
                pe.wait_ge(ctx_out, min(4 * b + 4 + it, 4 * NB))
                for pr in range(NP):
                    last = pe.matmul(bank[:, out_bank(b, it), 0:D], ctxT[b % 2][:, pr, it * P:(it + 1) * P], NN[:, pr, :],
                                     start=(pr == 0), stop=(pr == NP - 1))
                last.then_inc(o_ready, 1)

            def moe(t, half_):
                b, it = t // 2, t % 2
                edges = (0, 416, 800, 1184, WM)
                for c in range(2 * half_, 2 * half_ + 2):
                    at = (2 * (t % 2) if half_ == 0 else 4) + c % 2
                    a, z = edges[c], edges[c + 1]
                    last = three(bank[:, at, 0:z - a],
                                 [(XH[:, b % 2, k, it * P:(it + 1) * P], XL[:, b % 2, k, it * P:(it + 1) * P],
                                   WHm[:, k, a:z], WLm[:, k, a:z]) for k in range(2)])
                last.then_inc(u_ready if half_ else g_ready, 1)

            def moe_gate(t):
                if t == 0:
                    pe.wait_ge(m_lo, 4)
                    pe.wait_ge(p_exp, UNITS - 1)
                if t == 1:
                    pe.wait_ge(p_exp, UNITS)
                if t % 2 == 0:
                    pe.wait_ge(ln_lo, 13 + t // 2)
                if t >= 2:
                    pe.wait_ge(at_out, t - 1)
                moe(t, 0)

            def moe_up(t):
                if t == 0:
                    pe.wait_ge(pt_out0, 32)
                    pe.wait_ge(pt_out1, 32)
                else:
                    pe.wait_ge(m_act, t)
                moe(t, 1)

            def act_transpose(t):
                pe.wait_ge(m_act, t + 1)
                for c in range(6):
                    last = pe.transpose(bank[:, 2 * (t % 2) + c // 3, (c % 3) * P:(c % 3 + 1) * P],
                                        actb[t % 2][:, c * P:(c + 1) * P], ident[:, :])
                last.then_inc(at_ready, 1)

            def moe_down(t):
                pe.wait_ge(at_out, t + 1)
                if t == 0:
                    pe.wait_ge(ld_dn, 16 * N_DN)
                    pe.wait_ge(o_out, 2 * NB - 1)
                else:
                    pe.wait_ge(x_out, t)
                for c in range(6):
                    last = pe.matmul(bank[:, 6, 0:D], actT[t % 2][:, c, :], dnT[:, c, :], start=(c == 0), stop=(c == 5))
                last.then_inc(dn_ready, 1)

            for c in range(4):
                queries(0, c)
            down(3, 0)
            scores(0)
            down(3, 1)
            for u in range(STEPS):
                if u in (UNITS, UNITS + 1):
                    moe_gate(u - UNITS)
                if 2 <= u <= UNITS + 1:
                    probs_transpose(u - 2)
                if 1 <= u < UNITS:
                    scores(u)
                if u < 24 and u % 2 == 1:
                    queries(u // 8 + 1, u % 8 // 2)
                if u in LN_STEPS:
                    ln_transpose(LN_STEPS[u])
                if u % 2 == 0 and 4 <= u <= UNITS + 2:
                    context((u - 4) // 2)
                if u == UNITS + 3:
                    moe_up(0)
                for b, it in OUT_STEPS.get(u, []):
                    attn_out(b, it)
            for t in range(8):
                if t:
                    moe_up(t)
                if t in (2, 4):
                    ln_transpose(13 + t // 2)
                if 1 <= t < 7:
                    moe_gate(t + 1)
                if t == 7:
                    moe_down(6)
                act_transpose(t)
                if 1 <= t < 7:
                    moe_down(t - 1)
            moe_down(7)


def layout(i):
    c = np.ascontiguousarray
    x, ctx = i["x"], i["ctx_512"]
    f = x.dtype
    ctxT = ctx.transpose(2, 0, 1).reshape(DC, NB * S)
    ctxA = np.concatenate([ctxT, np.ones((1, NB * S), f)])
    WkA = np.concatenate([i["L0_xattn_W_k"].T, i["L0_xattn_b_k"][None, :]])
    gu = np.stack([i["L0_ffn_w_gate"], i["L0_ffn_w_up"]])
    gu = gu.reshape(2, 2, P, S, 4).transpose(2, 1, 0, 4, 3)
    wd = i["L0_ffn_w_down"].reshape(2, P, 4, D).transpose(1, 0, 2, 3)
    kr = i["L1_xattn_W_kr"]
    krB = np.zeros((P, NP, P), f)
    for j in range(2):
        krB[64 * j:64 * j + 64, :, 64 * j:64 * j + 64] = kr[j::2].transpose(2, 0, 1)
    gup = i["L1_ffn_gate_up_proj"].reshape(NE, 2, EI, 2, P).transpose(0, 1, 4, 3, 2)
    inv = (np.float32(1.0) / np.float32(10000.0) ** (np.arange(0, DC, 2, dtype=np.float32) / np.float32(DC))).astype(np.float32)
    freq = np.arange(S, dtype=np.float32)[:, None] * inv[None, :]
    sin, cos = (np.repeat(g(freq), 2, axis=-1).astype(np.float32) for g in (np.sin, np.cos))
    sin = np.where(np.arange(DC) < DC // 2, -sin, sin).astype(np.float32)
    kN = ctx.reshape(NB * TT, P, DC).transpose(1, 0, 2)
    out = {
        "x": x, "ctxA": ctxA, "WkA": np.concatenate([WkA, WkA], axis=1), "ident": np.eye(P, dtype=np.float32),
        "gamma": i["L0_xattn_ln_gamma"], "beta": i["L0_xattn_ln_beta"],
        "wq": i["L1_xattn_Wq"].reshape(NH, HK, D).transpose(1, 0, 2),
        "kcq": i["L1_xattn_w_kc_q"].transpose(1, 0, 2),
        "qr": i["L1_xattn_W_qr"].reshape(NH, 2, 96, DC).transpose(2, 1, 0, 3),
        "krB": krB, "kckv": i["L1_xattn_w_kc_kv"].transpose(1, 0, 2),
        "woT": i["L1_xattn_Wo"].reshape(D, NH, HK).transpose(2, 1, 0),
        "wgu": gu.reshape(P, 4 * FFN), "wd": wd.reshape(P, 8, D),
        "kT": np.concatenate([ctxT, ctxT]), "kTrot": np.concatenate([np.roll(ctxT, 32, 0)] * 2),
        "cosT": np.concatenate([cos.T, cos.T]), "sinT": np.concatenate([sin.T, sin.T]),
        "kN": kN, "kNrot": np.roll(kN, 32, 2),
        "cosN": cos.reshape(TT, P, DC).transpose(1, 0, 2), "sinN": sin.reshape(TT, P, DC).transpose(1, 0, 2),
        "dom": i["L1_ffn_dominant_experts"].reshape(1, NG), "mg": i["L1_ffn_merge_groups"],
        "gwT": i["L1_ffn_gate_weight"].reshape(NE, 2, P).transpose(2, 1, 0),
        "gup": gup, "dn": i["L1_ffn_down_proj"].transpose(0, 2, 1),
    }
    return {k: c(v) for k, v in out.items()}


def kernel(**inputs):
    import concourse.bacc as bacc
    from concourse.bass_utils import run_bass_kernel_spmd

    arrays = layout({k: np.asarray(v) for k, v in inputs.items()})
    nc = bacc.Bacc("TRN2", target_bir_lowering=False, num_devices=1)
    ins = {k: nc.dram_tensor(f"in_{k}", v.shape, mybir.dt.from_np(v.dtype), kind="ExternalInput").ap()
           for k, v in arrays.items()}
    out = nc.dram_tensor("out_x", (NB, S, D), F32, kind="ExternalOutput").ap()
    two_layers(nc, ins, out)
    r = run_bass_kernel_spmd(nc, [{f"in_{k}": v for k, v in arrays.items()}], core_ids=[0])
    return r.results[0]["out_x"]
```
